# Optimizing a Trainium2 kernel written in Bass

```python
import numpy as np
import jax
import jax.numpy as jnp

def _softmax(x, axis=-1):
    return jax.nn.softmax(x, axis=axis)

def _gelu(x):
    return jax.nn.gelu(x, approximate=True)

def _silu(x):
    return jax.nn.silu(x)

def _sigmoid(x):
    return jax.nn.sigmoid(x)

def _layernorm(x, axis=-1, eps=1e-05):
    m = jnp.mean(x, axis=axis, keepdims=True)
    v = jnp.var(x, axis=axis, keepdims=True)
    return (x - m) / jnp.sqrt(v + eps)

def _scatter_add(tgt, idx, src, axis=0):
    return tgt.at[idx].add(src)

def _segment_sum(src, seg, n):
    return jax.ops.segment_sum(src, seg, n)
kernel_name = 'mk_cond_seq_d1_seqx_r2_3b6518'

def setup_inputs(seed: int=0):
    np.random.seed(seed)
    _w = jnp.asarray

    def _rec_inputs():
        import jax
        import jax.numpy as jnp
        _rk = jax.random.key(seed)
        x = -0.000125 + 0.9999 * jax.random.normal(jax.random.fold_in(_rk, 1), (4, 1024, 1024), jnp.float32)
        _lenS = 1024 - jax.random.randint(jax.random.fold_in(_rk, 7), (4,), 0, max(1, 1024 // 4) + 1, jnp.int32)
        _lenS2 = 1024 - jax.random.randint(jax.random.fold_in(_rk, 8), (4,), 0, max(1, 1024 // 4) + 1, jnp.int32)
        cond_2048 = 0.00782532 + 1.00527 * jax.random.normal(jax.random.fold_in(_rk, 11), (4, 1024), jnp.float32)
        return (x, cond_2048)
    x, cond_2048 = _rec_inputs()

    def _L0_cond_setup():
        import jax, jax.numpy as jnp
        import numpy as np
        B, T, LATENT, FFN, TEMB = (4, 2048, 128, 512, 1024)
        D = 8 * LATENT
        LN_EPS = 1e-05

        def _layernorm(h, g, b):
            mu = jnp.mean(h, axis=-1, keepdims=True)
            var = jnp.mean(jnp.square(h - mu), axis=-1, keepdims=True)
            return (h - mu) * jax.lax.rsqrt(var + LN_EPS) * g + b
        key = jax.random.key(seed)
        ks = jax.random.split(key, 12)
        s1 = 1.0 / np.sqrt(LATENT)
        s2 = 1.0 / np.sqrt(FFN)
        sd = 1.0 / np.sqrt(D)
        st = 1.0 / np.sqrt(TEMB)
        return {'x': jax.random.normal(ks[0], (B, T, D), dtype=jnp.float32), 'emb': jax.random.normal(ks[1], (B, TEMB), dtype=jnp.float32), 'W1': jax.random.uniform(ks[2], (8, LATENT, FFN), jnp.float32, -s1, s1), 'b1': jax.random.uniform(ks[3], (8, FFN), jnp.float32, -s1, s1), 'W2': jax.random.uniform(ks[4], (8, FFN, LATENT), jnp.float32, -s2, s2), 'b2': jax.random.uniform(ks[5], (8, LATENT), jnp.float32, -s2, s2), 'emb_W': jax.random.uniform(ks[6], (TEMB, 2 * D), jnp.float32, -st, st), 'emb_b': jax.random.uniform(ks[7], (2 * D,), jnp.float32, -st, st), 'ln_g': jnp.ones((D,), jnp.float32), 'ln_b': jnp.zeros((D,), jnp.float32), 'out_W': jax.random.uniform(ks[8], (D, D), jnp.float32, -sd, sd), 'out_b': jax.random.uniform(ks[9], (D,), jnp.float32, -sd, sd)}
    _L0_cond_all = _L0_cond_setup()
    _L0_cond_in = {k: v for k, v in _L0_cond_all.items() if k in ('W1', 'b1', 'W2', 'b2', 'emb_W', 'emb_b', 'ln_g', 'ln_b', 'out_W', 'out_b')}
    del _L0_cond_all
    return {'x': x, 'cond_2048': cond_2048, 'L0_cond_W1': _L0_cond_in['W1'], 'L0_cond_b1': _L0_cond_in['b1'], 'L0_cond_W2': _L0_cond_in['W2'], 'L0_cond_b2': _L0_cond_in['b2'], 'L0_cond_emb_W': _L0_cond_in['emb_W'], 'L0_cond_emb_b': _L0_cond_in['emb_b'], 'L0_cond_ln_g': _L0_cond_in['ln_g'], 'L0_cond_ln_b': _L0_cond_in['ln_b'], 'L0_cond_out_W': _L0_cond_in['out_W'], 'L0_cond_out_b': _L0_cond_in['out_b']}

def reference(x, cond_2048, L0_cond_W1, L0_cond_b1, L0_cond_W2, L0_cond_b2, L0_cond_emb_W, L0_cond_emb_b, L0_cond_ln_g, L0_cond_ln_b, L0_cond_out_W, L0_cond_out_b):
    import jax
    import jax.numpy as jnp

    def _L0_cond_ref(x, emb, W1, b1, W2, b2, emb_W, emb_b, ln_g, ln_b, out_W, out_b):
        import jax, jax.numpy as jnp
        import numpy as np
        B, T, LATENT, FFN, TEMB = (4, 2048, 128, 512, 1024)
        D = 8 * LATENT
        LN_EPS = 1e-05

        def _layernorm(h, g, b):
            mu = jnp.mean(h, axis=-1, keepdims=True)
            var = jnp.mean(jnp.square(h - mu), axis=-1, keepdims=True)
            return (h - mu) * jax.lax.rsqrt(var + LN_EPS) * g + b
        Bx, Tx, Dx = x.shape
        xr = x.reshape(Bx, Tx, 8, LATENT)
        h = jnp.einsum('btel,elf->btef', xr, W1) + b1
        h = jax.nn.gelu(h, approximate=False)
        y = jnp.einsum('btef,efl->btel', h, W2) + b2
        y = y.reshape(Bx, Tx, Dx)
        eo = jax.nn.silu(emb) @ emb_W + emb_b
        scale, shift = jnp.split(eo[:, None, :], 2, axis=-1)
        hn = _layernorm(y, ln_g, ln_b) * (1.0 + scale) + shift
        proj = jax.nn.silu(hn) @ out_W + out_b
        return x + proj
    x = _L0_cond_ref(x, cond_2048, L0_cond_W1, L0_cond_b1, L0_cond_W2, L0_cond_b2, L0_cond_emb_W, L0_cond_emb_b, L0_cond_ln_g, L0_cond_ln_b, L0_cond_out_W, L0_cond_out_b)
    return x

_drawn_inputs = setup_inputs


def setup_inputs(seed=0):
    import zlib

    import numpy as np

    out = dict(_drawn_inputs(seed))
    spreads = {'L0_cond_ln_g': (1.0, 0.2), 'L0_cond_ln_b': (0.0, 0.1)}
    factors = {'L0_cond_emb_b': 6.371, 'L0_cond_out_b': 3.407}
    for name, (base, spread) in spreads.items():
        noise = np.random.default_rng([zlib.crc32(name.encode()), seed]).standard_normal(out[name].shape)
        drawn = base * np.exp(spread * noise) if base else spread * noise
        out[name] = jnp.asarray(drawn.astype(out[name].dtype))
    for name, factor in factors.items():
        out[name] = (out[name] * factor).astype(out[name].dtype)
    return out
```

```python
from contextlib import ExitStack

import concourse.bass as bass
from concourse import mybir

P = 128
F32 = mybir.dt.float32
F32R = mybir.dt.float32r
ALU = mybir.AluOpType
ACT = mybir.ActivationFunctionType

BANK = 512
LN_EPS = 1e-5


def cond_ffn_program(nc, x, cond, W1, b1, W2, b2, emb_W, emb_b, ln_g, ln_b, out_W, out_b, out):
    B, T, D = x.shape
    G, L, FF = W1.shape
    C = FF // P
    KE = cond.shape[1] // P
    NE = emb_W.shape[1] // P
    TA = T
    SUB = TA // P
    NA = B * T // TA
    TB = BANK
    H = TA // TB
    NB = B * T // TB
    SB = TB // P
    K = G * C
    assert L == P and D == G * L and TA == 2 * BANK and D == 2 * BANK and G % 2 == 0 and C == 4

    y_scratch = nc.dram_tensor("y_scratch", [NB, P, G, TB], F32, kind="Internal").ap()

    R_B1 = 0
    R_B2 = R_B1 + G * C
    R_EB = R_B2 + G
    R_G = R_EB + NE
    R_B = R_G + G
    R_C = R_B + G
    ROWS = R_C + B * KE
    assert ROWS <= P

    with ExitStack() as ctx:
        def sb(name, shape, dt=F32, scope=ctx):
            return scope.enter_context(nc.sbuf_tensor(name, shape, dt))

        def sem(name):
            return ctx.enter_context(nc.semaphore(name))

        psum = ctx.enter_context(nc.psum_tensor("psum", [P, 8, BANK], F32))

        oW_hi = sb("oW_hi", [P, G, D], F32R)
        oW_lo = sb("oW_lo", [P, G, D], F32R)
        ident = sb("ident", [P, P])
        vec_rows = sb("vec_rows", [P, P])
        cols = sb("cols", [P, ROWS])
        out_b_all = sb("out_b_all", [P, D])

        sp_waits = sem("sp_waits")

        ident_zeroed = sem("ident_zeroed")
        ident_ready = sem("ident_ready")
        vec_landed = sem("vec_landed")
        vec_turned = sem("vec_turned")
        cols_ready = sem("cols_ready")
        out_b_landed = sem("out_b_landed")
        wraw_landed = [sem(f"wraw_landed{s}") for s in range(2)]
        praw_landed = [sem(f"praw_landed{s}") for s in range(2)]
        w_hi_done = sem("w_hi_done")
        w_split0 = sem("w_split0")
        pw_hi_done = sem("pw_hi_done")
        pw_split = sem("pw_split")

        x_landed = [sem(f"x_landed{s}") for s in range(2)]
        xT_psum = sem("xT_psum")
        xhi_done = sem("xhi_done")
        xlo_done = sem("xlo_done")
        s1_done = sem("s1_done")
        gelu_done = sem("gelu_done")
        ghi_done = sem("ghi_done")
        glo_done = sem("glo_done")
        s2_done = sem("s2_done")
        y_psum_free = sem("y_psum_free")
        y_staged = sem("y_staged")
        y_stored = [sem(f"y_stored{s}") for s in range(2)]

        with ExitStack() as ctx_a:
            W1_hi = sb("W1_hi", [P, G, FF], F32R, ctx_a)
            W1_lo = sb("W1_lo", [P, G, FF], F32R, ctx_a)
            W2_hi = sb("W2_hi", [P, G, FF], F32R, ctx_a)
            W2_lo = sb("W2_lo", [P, G, FF], F32R, ctx_a)
            wraw = sb("wraw", [P, 2, 2 * FF], F32, ctx_a)
            xin = sb("xin", [P, 2, SUB, P], F32, ctx_a)
            xT_hi = sb("xT_hi", [P, 2, TA], F32R, ctx_a)
            xT_lo = sb("xT_lo", [P, 2, TA], F32R, ctx_a)
            g_raw = sb("g_raw", [P, 2, TA], F32, ctx_a)
            g_hi = sb("g_hi", [P, 2, TA], F32R, ctx_a)
            g_lo = sb("g_lo", [P, 2, TA], F32R, ctx_a)
            y_stage = sb("y_stage", [P, 2, TA], F32, ctx_a)
            assert D == 2 * FF

            def ring(s):
                return psum[:, 2 * s:2 * s + 2, :].rearrange("p b n -> p (b n)")

            def y_psum(s):
                return psum[:, 4 + 2 * s:6 + 2 * s, :].rearrange("p b n -> p (b n)")

            def slot_T(k):
                return (3 + k + k // C) % 2

            def slot_S1(k):
                return (3 + k + k // C + 1) % 2

            x_cols = x.rearrange("b (s p) (g l) -> b g p s l", p=P, l=L)
            y_out = y_scratch.rearrange("(i h) p g t -> i g p h t", h=H)

            block = ctx_a.enter_context(nc.Block())

            @block.sync
            def _(sp):
                def wait(signal, value):
                    sp.wait_ge(signal, value)
                    sp.sem_inc(sp_waits, 1)

                def load_x(i, n_i, g):
                    sp.dma_start(xin[:, g % 2], x_cols[i, g]).then_inc(x_landed[g % 2], 16)

                load_x(0, 0, 0)
                for r0, v in ((R_B1, b1.rearrange("g (c p) -> (g c) p", p=P)), (R_B2, b2),
                              (R_EB, emb_b.rearrange("(n p) -> n p", p=P)),
                              (R_G, ln_g.rearrange("(n p) -> n p", p=P)),
                              (R_B, ln_b.rearrange("(n p) -> n p", p=P)),
                              (R_C, cond.rearrange("b (k p) -> (b k) p", p=P))):
                    sp.dma_start(vec_rows[r0:r0 + v.shape[0], :], v).then_inc(vec_landed, 16)
                load_x(0, 0, 1)
                sp.dma_start(out_b_all[:], out_b.rearrange("(o d) -> o d", o=1).to_broadcast([P, D])
                             ).then_inc(out_b_landed, 16)

                def body(i, last):
                    for g in range(G):
                        if not (last and g + 2 >= G):
                            wait(xT_psum, G * i + g + 1)
                            if g + 2 < G:
                                load_x(i, i, g + 2)
                            else:
                                load_x(i + 1, i + 1, g + 2 - G)
                        wait(y_staged, G * i + g + 1)
                        sp.dma_start(y_out[i, g], y_stage[:, g % 2].rearrange("p (h t) -> p h t", h=H)
                                     ).then_inc(y_stored[g % 2], 16)

                with sp.Fori(0, NA - 1) as i:
                    body(i, False)
                body(NA - 1, True)
                for s in range(2):
                    sp.wait_ge(y_stored[s], 16 * NA * G // 2)

            @block.gpsimd
            def _(pool):
                nc.gpsimd.memset(ident[:], 0.0).then_inc(ident_zeroed, 1)
                pool.wait_ge(ident_zeroed, 1)
                nc.gpsimd.affine_select(out=ident[:], in_=ident[:], compare_op=ALU.not_equal, fill=1.0,
                                        base=0, pattern=[[-1, P]], channel_multiplier=1).then_inc(ident_ready, 1)

                def load(m):
                    s = m % 2
                    if m < G:
                        pool.dma_start(wraw[:, s, 0:FF], W1[m]).then_inc(praw_landed[s], 16)
                        pool.dma_start(wraw[:, s, FF:2 * FF].rearrange("p (c l) -> p c l", c=C),
                                       W2[m].rearrange("(c p) l -> p c l", p=P)).then_inc(praw_landed[s], 16)
                    else:
                        pool.dma_start(wraw[:, s, :], out_W[(m - G) * P:(m - G + 1) * P, :]
                                       ).then_inc(praw_landed[s], 16)

                def landed(m):
                    return 16 * sum(2 if n < G else 1 for n in range(2 + m % 2, m + 1, 2))

                pool.wait_ge(w_split0, 2)
                load(2)
                for m in range(1, 2 * G):
                    s = m % 2
                    if m == 1:
                        pool.wait_ge(wraw_landed[1], 32)
                    else:
                        pool.wait_ge(praw_landed[s], landed(m))
                    if m < G:
                        parts = ((W1_hi[:, m], W1_lo[:, m], wraw[:, s, 0:FF]),
                                 (W2_hi[:, m], W2_lo[:, m], wraw[:, s, FF:2 * FF]))
                    else:
                        parts = tuple((oW_hi[:, m - G, a:a + FF], oW_lo[:, m - G, a:a + FF],
                                       wraw[:, s, a:a + FF]) for a in (0, FF))
                    for j, (hi, lo, raw) in enumerate(parts):
                        nc.gpsimd.tensor_copy(hi, raw).then_inc(pw_hi_done, 1)
                        pool.wait_ge(pw_hi_done, 2 * (m - 1) + j + 1)
                        nc.gpsimd.tensor_tensor(lo, raw, hi.bitcast(F32), ALU.subtract).then_inc(pw_split, 1)
                    if m + 2 < 2 * G:
                        pool.wait_ge(pw_split, 2 * m)
                        load(m + 2)

            @block.scalar
            def _(act):
                for m in range(2):
                    act.dma_start(wraw[:, m, 0:FF], W1[m]).then_inc(wraw_landed[m], 16)
                    act.dma_start(wraw[:, m, FF:2 * FF].rearrange("p (c l) -> p c l", c=C),
                                  W2[m].rearrange("(c p) l -> p c l", p=P)).then_inc(wraw_landed[m], 16)
                act.sem_inc(y_psum_free, 2)

                def round_xT(n, slot, g):
                    act.wait_ge(xT_psum, n + 1)
                    nc.scalar.copy(xT_hi[:, g % 2], ring(slot)).then_inc(xhi_done, 1)

                def gelu(m, k, slot):
                    act.wait_ge(s1_done, m + 1)
                    nc.scalar.activation(g_raw[:, k % 2], ring(slot), ACT.Gelu,
                                         bias=cols[:, R_B1 + k:R_B1 + k + 1]).then_inc(gelu_done, 1)

                round_xT(0, 0, 0)
                act.wait_ge(cols_ready, 1)
                gelu(0, 0, 1)
                gelu(1, 1, 0)

                def body(i, last):
                    for k in range(K):
                        g = k // C
                        if k % C == 0 and not (last and g + 1 == G):
                            round_xT(G * i + g + 1, slot_T(k), (g + 1) % G)
                        if not (last and k + 2 >= K):
                            act.wait_ge(glo_done, K * i + k + 1)
                            gelu(K * i + k + 2, (k + 2) % K, slot_S1(k))
                        if k % C == C - 1:
                            act.wait_ge(s2_done, K * i + k + 1)
                            act.wait_ge(y_stored[g % 2], 16 * ((G // 2) * i + g // 2))
                            nc.scalar.activation(y_stage[:, g % 2], y_psum(g % 2), ACT.Identity,
                                                 bias=cols[:, R_B2 + g:R_B2 + g + 1]).then_inc(y_staged, 1)
                            act.wait_ge(y_staged, G * i + g + 1)
                            act.sem_inc(y_psum_free, 1)

                with act.Fori(0, NA - 1) as i:
                    body(i, False)
                body(NA - 1, True)

            @block.vector
            def _(dve):
                dve.wait_ge(wraw_landed[0], 32)
                for j, (hi, lo) in enumerate(((W1_hi, W1_lo), (W2_hi, W2_lo))):
                    raw = wraw[:, 0, j * FF:(j + 1) * FF]
                    nc.vector.tensor_copy(hi[:, 0], raw).then_inc(w_hi_done, 1)
                    dve.wait_ge(w_hi_done, j + 1)
                    nc.vector.tensor_tensor(lo[:, 0], raw, hi[:, 0].bitcast(F32), ALU.subtract
                                            ).then_inc(w_split0, 1)
                dve.wait_ge(vec_turned, 1)
                nc.vector.tensor_copy(cols[:], psum[:, 4, 0:ROWS]).then_inc(cols_ready, 1)

                def rest_xT(n, slot, g):
                    dve.wait_ge(xhi_done, n + 1)
                    nc.vector.tensor_tensor(xT_lo[:, g % 2], ring(slot), xT_hi[:, g % 2].bitcast(F32),
                                            ALU.subtract).then_inc(xlo_done, 1)

                def split_gelu(m, s):
                    dve.wait_ge(gelu_done, m + 1)
                    nc.vector.tensor_copy(g_hi[:, s], g_raw[:, s]).then_inc(ghi_done, 1)
                    dve.wait_ge(ghi_done, m + 1)
                    nc.vector.tensor_tensor(g_lo[:, s], g_raw[:, s], g_hi[:, s].bitcast(F32),
                                            ALU.subtract).then_inc(glo_done, 1)

                rest_xT(0, 0, 0)
                split_gelu(0, 0)
                split_gelu(1, 1)

                def body(i, last):
                    for k in range(K):
                        g = k // C
                        if k % C == 0 and not (last and g + 1 == G):
                            rest_xT(G * i + g + 1, slot_T(k), (g + 1) % G)
                        if not (last and k + 2 >= K):
                            dve.wait_ge(s2_done, K * i + k + 1)
                            split_gelu(K * i + k + 2, k % 2)

                with dve.Fori(0, NA - 1) as i:
                    body(i, False)
                body(NA - 1, True)

            @block.tensor
            def _(pe):
                def turn_x(slot, g):
                    for s in range(SUB):
                        mm = nc.tensor.transpose(ring(slot)[:, s * P:(s + 1) * P], xin[:, g % 2, s], ident[:])
                    mm.then_inc(xT_psum, 1)

                def first(k, slot):
                    g, c = k // C, k % C
                    cut = slice(c * P, (c + 1) * P)
                    for n, (w, v) in enumerate(((W1_hi, xT_hi), (W1_lo, xT_hi), (W1_hi, xT_lo))):
                        for h in range(2):
                            mm = nc.tensor.matmul(ring(slot)[:, h * BANK:(h + 1) * BANK], w[:, g, cut],
                                                  v[:, g % 2, h * BANK:(h + 1) * BANK],
                                                  start=(n == 0), stop=(n == 2))
                    mm.then_inc(s1_done, 1)

                def second(k):
                    g, c = k // C, k % C
                    cut = slice(c * P, (c + 1) * P)
                    for n, (w, v) in enumerate(((W2_hi, g_hi), (W2_lo, g_hi), (W2_hi, g_lo))):
                        for h in range(2):
                            mm = nc.tensor.matmul(y_psum(g % 2)[:, h * BANK:(h + 1) * BANK], w[:, g, cut],
                                                  v[:, k % 2, h * BANK:(h + 1) * BANK],
                                                  start=(c == 0 and n == 0), stop=(c == C - 1 and n == 2))
                    mm.then_inc(s2_done, 1)

                pe.wait_ge(ident_ready, 1)
                pe.wait_ge(x_landed[0], 16)
                turn_x(0, 0)
                pe.wait_ge(vec_landed, 16 * 6)
                nc.tensor.transpose(psum[:, 4, 0:ROWS], vec_rows[0:ROWS, :], ident[0:ROWS, 0:ROWS]
                                    ).then_inc(vec_turned, 1)
                pe.wait_ge(w_split0, 2)
                pe.wait_ge(xlo_done, 1)
                first(0, 1)
                first(1, 0)

                def body(i, last):
                    for k in range(K):
                        g = k // C
                        n = G * i + g
                        if k % C == 0 and not (last and g + 1 == G):
                            if g + 1 < G:
                                pe.wait_ge(x_landed[(g + 1) % 2], 16 * ((G // 2) * i + (g + 1) // 2 + 1))
                            else:
                                pe.wait_ge(x_landed[0], 16 * ((G // 2) * i + G // 2 + 1))
                            pe.wait_ge(gelu_done, K * i + k + 1)
                            turn_x(slot_T(k), (g + 1) % G)
                        if not (last and k + 2 >= K):
                            if k % C == 0:
                                pe.wait_ge(gelu_done, K * i + k + 2)
                            elif k % C == 1 and not (last and g + 1 == G):
                                pe.wait_ge(xlo_done, n + 2)
                            else:
                                pe.wait_ge(gelu_done, K * i + k + 1)
                            if k % C == C - 2:
                                pe.wait_ge(xlo_done, n + 2)
                                if g + 1 < G:
                                    pe.wait_ge(pw_split, 2 * (g + 1))
                            first((k + 2) % K, slot_S1(k))
                        pe.wait_ge(glo_done, K * i + k + 1)
                        if k % C == 0:
                            pe.wait_ge(y_psum_free, n + 1)
                        second(k)

                with pe.Fori(0, NA - 1) as i:
                    body(i, False)
                body(NA - 1, True)

        emb_landed = [sem(f"emb_landed{s}") for s in range(4)]
        silu_cond_done = sem("silu_cond_done")
        emb_chunk = sem("emb_chunk")
        emb_step = sem("emb_step")
        ones_set = sem("ones_set")
        ones_ready = sem("ones_ready")
        y_landed = [sem(f"y_landed{s}") for s in range(2)]
        tree = sem("tree")
        sum_split = sem("sum_split")
        stat_psum = sem("stat_psum")
        centred = sem("centred")
        squared = sem("squared")
        std_done = sem("std_done")
        rstd_done = sem("rstd_done")
        normed = sem("normed")
        silu_done = sem("silu_done")
        shi_done = sem("shi_done")
        slo_done = sem("slo_done")
        proj_done = sem("proj_done")
        res_landed = [sem(f"res_landed{s}") for s in range(2)]
        res_biased = sem("res_biased")
        out_ready = sem("out_ready")
        out_stored = [sem(f"out_stored{s}") for s in range(2)]

        with ExitStack() as ctx_b:
            yb = sb("yb", [P, 2, G, TB], F32, ctx_b)
            sq = sb("sq", [P, G, TB], F32, ctx_b)
            s_hi = sb("s_hi", [P, 2, G, TB], F32R, ctx_b)
            s_lo = sb("s_lo", [P, 2, G, TB], F32R, ctx_b)
            sum_hi = sb("sum_hi", [P, TB], F32R, ctx_b)
            sum_lo = sb("sum_lo", [P, TB], F32R, ctx_b)
            std = sb("std", [P, TB], F32, ctx_b)
            rstd = sb("rstd", [P, TB], F32, ctx_b)
            res = sb("res", [P, 2, D], F32, ctx_b)
            ones = sb("ones", [P, P], F32, ctx_b)
            ones_r = sb("ones_r", [P, P], F32R, ctx_b)
            eps = sb("eps", [P, 1], F32, ctx_b)
            cond_silu = sb("cond_silu", [P, B * KE], F32, ctx_b)
            emb = sb("emb", [P, NE, B], F32, ctx_b)
            emb2 = sb("emb2", [P, NE, B], F32, ctx_b)
            mod_a = sb("mod_a", [P, B, G], F32, ctx_b)
            mod_c = sb("mod_c", [P, B, G], F32, ctx_b)
            mod_t = sb("mod_t", [P, B, G], F32, ctx_b)
            emb_w = yb[:, 1].rearrange("p (s r) (k q) -> p s (r k) q", s=4, q=P)

            HG = G // 2
            proj = [psum[:, 2 * s:2 * s + 2, :].rearrange("p b n -> p (b n)") for s in range(2)]
            mean_ps = psum[:, 4]
            var_ps = psum[:, 5]
            emb_ps = psum[:, 6, 0:NE * B]
            x_rows = x.rearrange("b (h s p) d -> (b h) s p d", p=P, s=SB)
            out_rows = out.rearrange("b (h s p) d -> (b h) s p d", p=P, s=SB)
            emb_chunks = emb_W.rearrange("(k p) (n q) -> n p k q", p=P, q=P)

            block = ctx_b.enter_context(nc.Block())

            @block.sync
            def _(sp):
                def wait(signal, value):
                    sp.wait_ge(signal, value)
                    sp.sem_inc(sp_waits, 1)

                sp.dma_start(yb[:, 0], y_scratch[0]).then_inc(y_landed[0], 16)
                for n in range(NE):
                    if n >= 4:
                        sp.wait_ge(emb_chunk, n - 3)
                    sp.dma_start(emb_w[:, n % 4], emb_chunks[n]).then_inc(emb_landed[n % 4], 16)
                sp.wait_ge(emb_chunk, NE)
                sp.dma_start(yb[:, 1], y_scratch[1]).then_inc(y_landed[1], 16)

                def load_y(i, s):
                    wait(slo_done, 2 * (i - 1))
                    sp.dma_start(yb[:, s], y_scratch[i]).then_inc(y_landed[s], 16)

                def load_res(i, t, s):
                    sp.dma_start(res[:, s], x_rows[i, t]).then_inc(res_landed[s], 16)

                def store(i, t):
                    wait(out_ready, SB * i + t + 1)
                    sp.dma_start(out_rows[i, t], res[:, t % 2]).then_inc(out_stored[t % 2], 16)

                load_res(0, 0, 0)
                load_res(0, 1, 1)

                def window(i, s, last):
                    for t in range(SB):
                        store(i, t)
                        if not (last and t + 2 >= SB):
                            wait(out_stored[t % 2], 16 * ((SB // 2) * i + t // 2 + 1))
                            load_res(i + (t + 2) // SB, (t + 2) % SB, t % 2)

                def pair(j, last):
                    i = 2 * j
                    if not last:
                        load_y(i + 2, 0)
                    window(i, 0, False)
                    if not last:
                        load_y(i + 3, 1)
                    window(i + 1, 1, last)

                with sp.Fori(0, NB // 2 - 1) as j:
                    pair(j, False)
                pair(NB // 2 - 1, True)
                for s in range(2):
                    sp.wait_ge(out_stored[s], 16 * NB * SB // 2)

            @block.gpsimd
            def _(pool):
                pool.wait_ge(out_b_landed, 16)

                def bias_res(i, t):
                    pool.wait_ge(res_landed[t % 2], 16 * ((SB // 2) * i + t // 2 + 1))
                    nc.gpsimd.tensor_tensor(res[:, t % 2], res[:, t % 2], out_b_all[:], ALU.add
                                            ).then_inc(res_biased, 1)

                with pool.Fori(0, NB) as i:
                    for t in range(SB):
                        bias_res(i, t)

            @block.scalar
            def _(act):
                nc.scalar.activation(cond_silu[:], cols[:, R_C:R_C + B * KE], ACT.Silu
                                     ).then_inc(silu_cond_done, 1)

                def squares(i, s):
                    for a in range(2):
                        if a == 0:
                            act.wait_ge(centred, i + 1)
                        nc.scalar.activation(sq[:, a * HG:(a + 1) * HG], yb[:, s, a * HG:(a + 1) * HG],
                                             ACT.Square).then_inc(squared, 1)

                def root(i):
                    act.wait_ge(stat_psum, 2 * i + 2)
                    nc.scalar.activation(std[:], var_ps, ACT.Sqrt, bias=eps[:]).then_inc(std_done, 1)

                def silu(i, s, b):
                    for g in range(G):
                        if g % HG == 0:
                            act.wait_ge(normed, 2 * i + g // HG + 1)
                        nc.scalar.activation(yb[:, s, g], yb[:, s, g], ACT.Silu,
                                             scale=mod_a[:, b, g:g + 1], bias=mod_c[:, b, g:g + 1]
                                             ).then_inc(silu_done, 1)

                def norm(i, s, b):
                    squares(i, s)
                    root(i)
                    silu(i, s, b)

                act.wait_ge(ones_set, 2)
                squares(0, 0)
                root(0)
                act.wait_ge(emb_step, 5)
                silu(0, 0, 0)

                def pair(j, last):
                    norm(2 * j + 1, 1, j)
                    if not last:
                        norm(2 * j + 2, 0, j + 1)

                with act.Fori(0, NB // 2 - 1) as j:
                    pair(j, False)
                pair(NB // 2 - 1, True)

            @block.vector
            def _(dve):
                nc.vector.memset(ones[:], 1.0 / D).then_inc(ones_set, 1)
                nc.vector.memset(eps[:], LN_EPS).then_inc(ones_set, 1)
                dve.wait_ge(ones_set, 2)
                nc.vector.tensor_copy(ones_r[:], ones[:]).then_inc(ones_ready, 1)

                def group_sum(n, src):
                    nc.vector.tensor_tensor(sq[:, 0:4], src[:, 0:4], src[:, 4:8], ALU.add).then_inc(tree, 1)
                    dve.wait_ge(tree, 3 * n + 1)
                    nc.vector.tensor_tensor(sq[:, 0:2], sq[:, 0:2], sq[:, 2:4], ALU.add).then_inc(tree, 1)
                    dve.wait_ge(tree, 3 * n + 2)
                    nc.vector.tensor_tensor(sq[:, 0], sq[:, 0], sq[:, 1], ALU.add).then_inc(tree, 1)
                    dve.wait_ge(tree, 3 * n + 3)
                    nc.vector.tensor_copy(sum_hi[:], sq[:, 0]).then_inc(sum_split, 1)
                    dve.wait_ge(sum_split, 2 * n + 1)
                    nc.vector.tensor_tensor(sum_lo[:], sq[:, 0], sum_hi[:].bitcast(F32), ALU.subtract
                                            ).then_inc(sum_split, 1)

                def centre(i, s):
                    dve.wait_ge(stat_psum, 2 * i + 1)
                    nc.vector.tensor_tensor(yb[:, s], yb[:, s],
                                            mean_ps.unsqueeze(1).to_broadcast([P, G, TB]), ALU.subtract
                                            ).then_inc(centred, 1)

                def square_sum(i):
                    dve.wait_ge(squared, 2 * i + 2)
                    group_sum(2 * i + 1, sq)

                def inverse(i):
                    dve.wait_ge(std_done, i + 1)
                    nc.vector.reciprocal(rstd[:], std[:]).then_inc(rstd_done, 1)
                    dve.wait_ge(rstd_done, i + 1)

                def normalise(i, s, a):
                    half = yb[:, s, a * HG:(a + 1) * HG]
                    nc.vector.tensor_tensor(half, half, rstd[:].unsqueeze(1).to_broadcast([P, HG, TB]),
                                            ALU.mult).then_inc(normed, 1)

                def split_s(i, s, a):
                    half = slice(a * HG, (a + 1) * HG)
                    dve.wait_ge(silu_done, G * i + (a + 1) * HG)
                    nc.vector.tensor_copy(s_hi[:, s, half], yb[:, s, half]).then_inc(shi_done, 1)
                    dve.wait_ge(shi_done, 2 * i + a + 1)
                    nc.vector.tensor_tensor(s_lo[:, s, half], yb[:, s, half],
                                            s_hi[:, s, half].bitcast(F32), ALU.subtract
                                            ).then_inc(slo_done, 1)

                def finish(i, t):
                    dve.wait_ge(proj_done, SB * i + t + 1)
                    dve.wait_ge(res_biased, SB * i + t + 1)
                    nc.vector.tensor_tensor(res[:, t % 2], proj[t % 2], res[:, t % 2], ALU.add
                                            ).then_inc(out_ready, 1)

                dve.wait_ge(y_landed[0], 16)
                group_sum(0, yb[:, 0])
                centre(0, 0)
                square_sum(0)
                inverse(0)
                normalise(0, 0, 0)
                normalise(0, 0, 1)
                dve.wait_ge(emb_chunk, NE)
                nc.vector.tensor_copy(emb[:].rearrange("p n b -> p (n b)"), emb_ps).then_inc(emb_step, 1)
                dve.wait_ge(emb_step, 1)
                nc.vector.tensor_tensor(emb2[:], emb[:], cols[:, R_EB:R_EB + NE].unsqueeze(2).to_broadcast([P, NE, B]),
                                        ALU.add).then_inc(emb_step, 1)
                dve.wait_ge(emb_step, 2)
                scale = emb2[:, 0:G].rearrange("p g b -> p b g")
                shift = emb2[:, G:NE].rearrange("p g b -> p b g")
                g_all = cols[:, R_G:R_G + G].unsqueeze(1).to_broadcast([P, B, G])
                b_all = cols[:, R_B:R_B + G].unsqueeze(1).to_broadcast([P, B, G])
                nc.vector.scalar_tensor_tensor(out=mod_a[:], in0=scale, scalar=1.0, in1=g_all,
                                               op0=ALU.add, op1=ALU.mult).then_inc(emb_step, 1)
                nc.vector.scalar_tensor_tensor(out=mod_t[:], in0=scale, scalar=1.0, in1=b_all,
                                               op0=ALU.add, op1=ALU.mult).then_inc(emb_step, 1)
                dve.wait_ge(emb_step, 4)
                nc.vector.tensor_tensor(mod_c[:], mod_t[:], shift, ALU.add).then_inc(emb_step, 1)
                split_s(0, 0, 0)
                split_s(0, 0, 1)

                def window(i, s, landed, last):
                    n = i + 1
                    if not last:
                        dve.wait_ge(y_landed[s], 16 * landed)
                        group_sum(2 * n, yb[:, s])
                        centre(n, s)
                    finish(i, 0)
                    if not last:
                        square_sum(n)
                        inverse(n)
                    finish(i, 1)
                    if not last:
                        normalise(n, s, 0)
                        normalise(n, s, 1)
                        split_s(n, s, 0)
                    finish(i, 2)
                    if not last:
                        split_s(n, s, 1)
                    finish(i, 3)

                def pair(j, last):
                    window(2 * j, 1, j + 1, False)
                    window(2 * j + 1, 0, j + 2, last)

                with dve.Fori(0, NB // 2 - 1) as j:
                    pair(j, False)
                pair(NB // 2 - 1, True)

            @block.tensor
            def _(pe):
                def mean_of(i, which):
                    ps = (mean_ps, var_ps)[which]
                    pe.wait_ge(sum_split, 4 * i + 2 * which + 2)
                    nc.tensor.matmul(ps, ones_r[:], sum_hi[:], start=True, stop=False)
                    nc.tensor.matmul(ps, ones_r[:], sum_lo[:], start=False, stop=True).then_inc(stat_psum, 1)

                pe.wait_ge(ones_ready, 1)
                mean_of(0, 0)
                pe.wait_ge(silu_cond_done, 1)
                cond_k = cond_silu[:].rearrange("p (b k) -> p k b", b=B)

                def embed(n):
                    pe.wait_ge(emb_landed[n % 4], 16 * (n // 4 + 1))
                    for k in range(KE):
                        mm = nc.tensor.matmul(emb_ps[:, n * B:(n + 1) * B], emb_w[:, n % 4, k], cond_k[:, k],
                                              start=(k == 0), stop=(k == KE - 1))
                    mm.then_inc(emb_chunk, 1)

                for n in range(NE // 2):
                    embed(n)
                mean_of(0, 1)
                for n in range(NE // 2, NE):
                    embed(n)

                def project(i, s, t, g):
                    p = t % 2
                    cut = slice(t * P, (t + 1) * P)
                    for n, (v, w) in enumerate(((s_hi, oW_hi), (s_hi, oW_lo), (s_lo, oW_hi))):
                        for h in range(2):
                            mm = nc.tensor.matmul(proj[p][:, h * BANK:(h + 1) * BANK], v[:, s, g, cut],
                                                  w[:, g, h * BANK:(h + 1) * BANK],
                                                  start=(g == 0 and n == 0), stop=(g == G - 1 and n == 2))
                    if g == G - 1:
                        mm.then_inc(proj_done, 1)

                def window(i, s, first, last):
                    for t in range(SB):
                        if not (first and t < 2):
                            pe.wait_ge(out_ready, SB * i + t - 1)
                        for g in range(G):
                            if t == 0 and g % HG == 0:
                                pe.wait_ge(slo_done, 2 * i + g // HG + 1)
                            project(i, s, t, g)
                            if t == 0 and g == 4 and not last:
                                mean_of(i + 1, 0)
                            if t == 1 and g == 6 and not last:
                                mean_of(i + 1, 1)

                def pair(j, first, last):
                    window(2 * j, 0, first, False)
                    window(2 * j + 1, 1, False, last)

                pair(0, True, False)
                with pe.Fori(1, NB // 2 - 1) as j:
                    pair(j, False, False)
                pair(NB // 2 - 1, False, True)


_INS = ["x", "cond_2048", "L0_cond_W1", "L0_cond_b1", "L0_cond_W2", "L0_cond_b2", "L0_cond_emb_W",
        "L0_cond_emb_b", "L0_cond_ln_g", "L0_cond_ln_b", "L0_cond_out_W", "L0_cond_out_b"]


def kernel(**inputs):
    import numpy as _np
    import concourse.bacc as _bacc
    from concourse import mybir as _mybir
    from concourse.bass_utils import run_bass_kernel_spmd as _run

    nc = _bacc.Bacc("TRN2", target_bir_lowering=False, num_devices=1)
    arrays, args = {}, []
    for name in _INS:
        a = _np.ascontiguousarray(inputs[name])
        arrays[f"in_{name}"] = a
        args.append(nc.dram_tensor(f"in_{name}", a.shape, _mybir.dt.from_np(a.dtype), kind="ExternalInput").ap())
    args.append(nc.dram_tensor("out", arrays["in_x"].shape, F32, kind="ExternalOutput").ap())
    cond_ffn_program(nc, *args)
    r = _run(nc, [arrays], core_ids=[0])
    return r.results[0]["out"]
```

```python
from contextlib import ExitStack

import concourse.bass as bass
from concourse import mybir

P = 128
F32 = mybir.dt.float32
F32R = mybir.dt.float32r
ALU = mybir.AluOpType
ACT = mybir.ActivationFunctionType

BANK = 512
LN_EPS = 1e-5


def cond_ffn_program(nc, x, cond, W1, b1, W2, b2, emb_W, emb_b, ln_g, ln_b, out_W, out_b, out):
    B, T, D = x.shape
    G, L, FF = W1.shape
    C = FF // P
    KE = cond.shape[1] // P
    NE = emb_W.shape[1] // P
    TA = T
    SUB = TA // P
    NA = B * T // TA
    TB = BANK
    H = TA // TB
    NB = B * T // TB
    SB = TB // P
    K = G * C
    assert L == P and D == G * L and TA == 2 * BANK and D == 2 * BANK and G % 2 == 0 and C == 4

    y_scratch = nc.dram_tensor("y_scratch", [NB, P, G, TB], F32, kind="Internal").ap()

    R_B1 = 0
    R_B2 = R_B1 + G * C
    R_EB = R_B2 + G
    R_G = R_EB + NE
    R_B = R_G + G
    R_C = R_B + G
    ROWS = R_C + B * KE
    assert ROWS <= P

    with ExitStack() as ctx:
        def sb(name, shape, dt=F32, scope=ctx):
            return scope.enter_context(nc.sbuf_tensor(name, shape, dt))

        def sem(name):
            return ctx.enter_context(nc.semaphore(name))

        psum = ctx.enter_context(nc.psum_tensor("psum", [P, 8, BANK], F32))

        oW_hi = sb("oW_hi", [P, G, D], F32R)
        oW_lo = sb("oW_lo", [P, G, D], F32R)
        ident = sb("ident", [P, P])
        cols = sb("cols", [P, ROWS])
        ones_r = sb("ones_r", [P, P], F32R)
        eps = sb("eps", [P, 1])
        stat = sb("stat", [P, TB])
        sum_hi = sb("sum_hi", [P, TB], F32R)
        sum_lo = sb("sum_lo", [P, TB], F32R)
        cond_silu = sb("cond_silu", [P, KE, 32])
        emb_rows = sb("emb_rows", [P, BANK])
        vec_rows = emb_rows[:, 0:P]
        emb = sb("emb", [P, NE, B])
        mod_a = sb("mod_a", [P, B, G])
        mod_c = sb("mod_c", [P, B, G])
        mod_t = sb("mod_t", [P, B, G])

        with ExitStack() as a:
            W = sb("W", [P, G, 4, FF], F32R, a)
            xT_hi = sb("xT_hi", [P, 2, TA], F32R, a)
            xT_lo = sb("xT_lo", [P, 2, TA], F32R, a)
            g_raw = sb("g_raw", [P, 2, TA], F32, a)
            g_hi = sb("g_hi", [P, 2, TA], F32R, a)
            g_lo = sb("g_lo", [P, 2, TA], F32R, a)
            xT_raw = sb("xT_raw", [P, TA], F32, a)
            xin = sb("xin", [P, 2, SUB, P], F32, a)
            y_stage = sb("y_stage", [P, 2, TA], F32, a)
            wraw = sb("wraw", [P, 2, 2 * FF], F32, a)
            assert D == 2 * FF == KE * P

        with ExitStack() as b:
            yb0 = sb("yb0", [P, G, TB], F32, b)
            sq0 = sb("sq0", [P, G, TB], F32, b)
            s_hi0 = sb("s_hi0", [P, G, TB], F32R, b)
            sq = sb("sq", [P, G, TB], F32, b)
            yb1 = sb("yb1", [P, G, TB], F32, b)
            s_hi1 = sb("s_hi1", [P, G, TB], F32R, b)
            s_lo1 = sb("s_lo1", [P, G, TB], F32R, b)
            res = sb("res", [P, 2, D], F32, b)
            out_b_all = sb("out_b_all", [P, D], F32, b)
        with ExitStack() as b:
            sb("below_s_lo0", [P, G, TB], F32, b)
            s_lo0 = sb("s_lo0", [P, G, TB], F32R, b)
        yb = (yb0, yb1)
        s_hi = (s_hi0, s_hi1)
        s_lo = (s_lo0, s_lo1)
        W1_HI, W1_LO, W2_HI, W2_LO = range(4)
        HG = G // 2

        sp_waits = sem("sp_waits")

        ident_zeroed = sem("ident_zeroed")
        ident_ready = sem("ident_ready")
        vec_landed = sem("vec_landed")
        vec_turned = sem("vec_turned")
        cols_ready = sem("cols_ready")
        ones_set = sem("ones_set")
        ones_ready = sem("ones_ready")
        wraw_landed = [sem(f"wraw_landed{s}") for s in range(2)]
        praw_landed = [sem(f"praw_landed{s}") for s in range(2)]
        w_hi_done = sem("w_hi_done")
        w_split0 = sem("w_split0")
        pw_hi_done = sem("pw_hi_done")
        pw_split = sem("pw_split")
        silu_cond_done = sem("silu_cond_done")
        cond_zeroed = sem("cond_zeroed")
        emb_landed = sem("emb_landed")
        emb_chunk = sem("emb_chunk")
        emb_copied = sem("emb_copied")
        emb_turned = sem("emb_turned")
        mod_step = sem("mod_step")

        x_landed = [sem(f"x_landed{s}") for s in range(2)]
        xT_psum = sem("xT_psum")
        xraw_done = sem("xraw_done")
        xhi_done = sem("xhi_done")
        xlo_done = sem("xlo_done")
        s1_done = sem("s1_done")
        gelu_done = sem("gelu_done")
        ghi_done = sem("ghi_done")
        glo_done = sem("glo_done")
        s2_done = sem("s2_done")
        y_psum_free = sem("y_psum_free")
        y_staged = sem("y_staged")
        y_stored = [sem(f"y_stored{s}") for s in range(2)]

        y0_landed = sem("y0_landed")
        y0_sum = sem("y0_sum")
        y0_split = sem("y0_split")
        y0_stat = sem("y0_stat")
        y0_mean = sem("y0_mean")
        y0_centred = sem("y0_centred")
        y0_squared = sem("y0_squared")
        y0_var = sem("y0_var")
        y0_std = sem("y0_std")
        y0_rstd = sem("y0_rstd")
        y0_normed = sem("y0_normed")
        y0_silu = sem("y0_silu")
        y0_shi = sem("y0_shi")
        y0_slo = sem("y0_slo")

        y_landed = [sem(f"y_landed{s}") for s in range(2)]
        tree = sem("tree")
        sum_split = sem("sum_split")
        stat_psum = sem("stat_psum")
        centred = sem("centred")
        squared = sem("squared")
        std_done = sem("std_done")
        rstd_done = sem("rstd_done")
        normed = sem("normed")
        silu_done = sem("silu_done")
        shi_done = sem("shi_done")
        slo_done = sem("slo_done")
        proj_done = sem("proj_done")
        out_b_landed = sem("out_b_landed")
        res_landed = [sem(f"res_landed{s}") for s in range(2)]
        res_biased = sem("res_biased")
        out_ready = sem("out_ready")
        out_stored = [sem(f"out_stored{s}") for s in range(2)]

        def ring(s):
            return psum[:, 2 * s:2 * s + 2, :].rearrange("p b n -> p (b n)")

        def y_psum(s):
            return psum[:, 4 + 2 * s:6 + 2 * s, :].rearrange("p b n -> p (b n)")

        proj = [ring(0), ring(1)]
        mean_ps = psum[:, 4]
        var_ps = psum[:, 5]

        K_EMB = list(range(3, K - 2, 3))[:KE]
        K_TURN = K_EMB[-1] + 2
        K_Y0, K_MEAN, K_VAR = 8, 15, 24
        assert len(K_EMB) == KE and NE == 4 * BANK // P

        def ring_plan(last):
            uses = [("S", 0), ("S", 1)]
            for k in range(K):
                if k % C == 0 and not (last and k // C + 1 == G):
                    uses.append(("T", k // C + 1))
                if last and k in K_EMB:
                    uses.append(("E", K_EMB.index(k)))
                if last and k == K_TURN:
                    uses.append(("F", 0))
                if last and k == K_MEAN:
                    uses.append(("M", 0))
                if last and k == K_VAR:
                    uses.append(("V", 0))
                if not (last and k + 2 >= K):
                    uses.append(("S", k + 2))
            slot = {u: (j + 1) % 2 for j, u in enumerate(uses)}
            before = {u: uses[j - 2] for j, u in enumerate(uses) if j >= 2}
            return slot, before

        PLAN = {last: ring_plan(last) for last in (False, True)}

        x_cols = x.rearrange("b (s p) (g l) -> b g p s l", p=P, l=L)
        y_out = y_scratch.rearrange("(i h) p g t -> i g p h t", h=H)
        x_rows = x.rearrange("b (h s p) d -> (b h) s p d", p=P, s=SB)
        out_rows = out.rearrange("b (h s p) d -> (b h) s p d", p=P, s=SB)

        block = ctx.enter_context(nc.Block())

        @block.sync
        def _(sp):
            def wait(signal, value):
                sp.wait_ge(signal, value)
                sp.sem_inc(sp_waits, 1)

            def load_x(i, g):
                sp.dma_start(xin[:, g % 2], x_cols[i, g]).then_inc(x_landed[g % 2], 16)

            load_x(0, 0)
            for r0, v in ((R_B1, b1.rearrange("g (c p) -> (g c) p", p=P)), (R_B2, b2),
                          (R_EB, emb_b.rearrange("(n p) -> n p", p=P)),
                          (R_G, ln_g.rearrange("(n p) -> n p", p=P)),
                          (R_B, ln_b.rearrange("(n p) -> n p", p=P)),
                          (R_C, cond.rearrange("b (k p) -> (b k) p", p=P))):
                sp.dma_start(vec_rows[r0:r0 + v.shape[0], :], v).then_inc(vec_landed, 16)
            load_x(0, 1)

            def load_emb(r):
                sp.dma_start(wraw[:].rearrange("p s q -> p (s q)"), emb_W[r * P:(r + 1) * P, :]
                             ).then_inc(emb_landed, 16)

            def body(i, last):
                if last:
                    wait(pw_split, 2 * (2 * G - 1))
                    load_emb(0)
                for k in range(K):
                    g = k // C
                    if k % C == 0 and not (last and g + 2 >= G):
                        wait(xT_psum, G * i + g + 1)
                        if g + 2 < G:
                            load_x(i, g + 2)
                        else:
                            load_x(i + 1, g + 2 - G)
                    if last and k in K_EMB[:-1]:
                        r = K_EMB.index(k)
                        wait(emb_chunk, r + 1)
                        load_emb(r + 1)
                    if last and k == K_Y0:
                        wait(s2_done, K * i + 2 * C)
                        for s in range(2):
                            wait(y_stored[s], 16 * (G // 2 + 1))
                        sp.dma_start(yb[0][:], y_scratch[0]).then_inc(y0_landed, 16)
                    if last and k == K - 2:
                        wait(s1_done, K * NA)
                        sp.dma_start(yb[1][:], y_scratch[1]).then_inc(y_landed[1], 16)
                    if k % C == C - 1:
                        wait(y_staged, G * i + g + 1)
                        sp.dma_start(y_out[i, g], y_stage[:, g % 2].rearrange("p (h t) -> p h t", h=H)
                                     ).then_inc(y_stored[g % 2], 16)

            with sp.Fori(0, NA - 1) as i:
                body(i, False)
            body(NA - 1, True)
            for s in range(2):
                wait(y_stored[s], 16 * (NA * G // 2 + 1))

            def load_res(i, t):
                sp.dma_start(res[:, t % 2], x_rows[i, t]).then_inc(res_landed[t % 2], 16)

            sp.dma_start(out_b_all[:], out_b.rearrange("(o d) -> o d", o=1).to_broadcast([P, D])
                         ).then_inc(out_b_landed, 16)
            load_res(0, 0)
            load_res(0, 1)
            wait(y0_slo, HG)
            sp.dma_start(yb[0][:], y_scratch[2]).then_inc(y_landed[0], 16)

            def window(i, w, load, last):
                for t in range(SB):
                    wait(out_ready, SB * i + t + 1)
                    sp.dma_start(out_rows[i, t], res[:, t % 2]).then_inc(out_stored[t % 2], 16)
                    if not (last and t + 2 >= SB):
                        wait(out_stored[t % 2], 16 * ((SB // 2) * i + t // 2 + 1))
                        load_res(i + (t + 2) // SB, (t + 2) % SB)
                if load:
                    s = (w + 1) % 2
                    wait(slo_done, 2 * i + 2)
                    sp.dma_start(yb[s][:], y_scratch[i + 3]).then_inc(y_landed[s], 16)

            with sp.Fori(0, NB // 2 - 2) as j:
                window(2 * j, 0, True, False)
                window(2 * j + 1, 1, True, False)
            for i in range(NB - 4, NB):
                window(i, i % 2, i + 3 < NB, i == NB - 1)
            for s in range(2):
                wait(out_stored[s], 16 * NB * SB // 2)

        @block.gpsimd
        def _(pool):
            nc.gpsimd.memset(ident[:], 0.0).then_inc(ident_zeroed, 1)
            pool.wait_ge(ident_zeroed, 1)
            nc.gpsimd.affine_select(out=ident[:], in_=ident[:], compare_op=ALU.not_equal, fill=1.0,
                                    base=0, pattern=[[-1, P]], channel_multiplier=1).then_inc(ident_ready, 1)

            def load(m):
                s = m % 2
                if m < G:
                    pool.dma_start(wraw[:, s, 0:FF], W1[m]).then_inc(praw_landed[s], 16)
                    pool.dma_start(wraw[:, s, FF:2 * FF].rearrange("p (c l) -> p c l", c=C),
                                   W2[m].rearrange("(c p) l -> p c l", p=P)).then_inc(praw_landed[s], 16)
                else:
                    pool.dma_start(wraw[:, s, :], out_W[(m - G) * P:(m - G + 1) * P, :]
                                   ).then_inc(praw_landed[s], 16)

            def landed(m):
                return 16 * sum(2 if n < G else 1 for n in range(2 + m % 2, m + 1, 2))

            pool.wait_ge(w_split0, 2)
            load(2)
            for m in range(1, 2 * G):
                s = m % 2
                if m == 1:
                    pool.wait_ge(wraw_landed[1], 32)
                else:
                    pool.wait_ge(praw_landed[s], landed(m))
                if m < G:
                    parts = ((W[:, m, W1_HI], W[:, m, W1_LO], wraw[:, s, 0:FF]),
                             (W[:, m, W2_HI], W[:, m, W2_LO], wraw[:, s, FF:2 * FF]))
                else:
                    parts = tuple((oW_hi[:, m - G, c:c + FF], oW_lo[:, m - G, c:c + FF],
                                   wraw[:, s, c:c + FF]) for c in (0, FF))
                for j, (hi, lo, raw) in enumerate(parts):
                    nc.gpsimd.tensor_copy(hi, raw).then_inc(pw_hi_done, 1)
                    pool.wait_ge(pw_hi_done, 2 * (m - 1) + j + 1)
                    nc.gpsimd.tensor_tensor(lo, raw, hi.bitcast(F32), ALU.subtract).then_inc(pw_split, 1)
                if m + 2 < 2 * G:
                    pool.wait_ge(pw_split, 2 * m)
                    load(m + 2)

            def split_sum(n):
                nc.gpsimd.tensor_copy(sum_hi[:], stat[:]).then_inc(y0_split, 1)
                pool.wait_ge(y0_split, 2 * n + 1)
                nc.gpsimd.tensor_tensor(sum_lo[:], stat[:], sum_hi[:].bitcast(F32), ALU.subtract
                                        ).then_inc(y0_split, 1)

            pool.wait_ge(y0_landed, 16)
            for g in range(1, G):
                if g > 1:
                    pool.wait_ge(y0_sum, g - 1)
                nc.gpsimd.tensor_tensor(stat[:], yb0[:, 0] if g == 1 else stat[:], yb0[:, g], ALU.add
                                        ).then_inc(y0_sum, 1)
            pool.wait_ge(y0_sum, G - 1)
            split_sum(0)
            pool.wait_ge(y0_mean, 1)
            for g in range(G):
                nc.gpsimd.tensor_tensor(yb0[:, g], yb0[:, g], stat[:], ALU.subtract).then_inc(y0_centred, 1)
            pool.wait_ge(y0_centred, G)
            for g in range(1, G):
                pool.wait_ge(y0_squared, g // 2 + 1)
                if g > 1:
                    pool.wait_ge(y0_sum, G - 1 + g - 1)
                nc.gpsimd.tensor_tensor(stat[:], sq0[:, 0] if g == 1 else stat[:], sq0[:, g], ALU.add
                                        ).then_inc(y0_sum, 1)
            pool.wait_ge(y0_sum, 2 * (G - 1))
            pool.wait_ge(y0_stat, 1)
            split_sum(1)
            pool.wait_ge(y0_rstd, 3)
            for g in range(G):
                nc.gpsimd.tensor_tensor(yb0[:, g], yb0[:, g], stat[:], ALU.mult).then_inc(y0_normed, 1)

            pool.wait_ge(out_b_landed, 16)
            with pool.Fori(0, NB) as i:
                for t in range(SB):
                    pool.wait_ge(res_landed[t % 2], 16 * ((SB // 2) * i + t // 2 + 1))
                    nc.gpsimd.tensor_tensor(res[:, t % 2], res[:, t % 2], out_b_all[:], ALU.add
                                            ).then_inc(res_biased, 1)

        @block.scalar
        def _(act):
            for m in range(2):
                act.dma_start(wraw[:, m, 0:FF], W1[m]).then_inc(wraw_landed[m], 16)
                act.dma_start(wraw[:, m, FF:2 * FF].rearrange("p (c l) -> p c l", c=C),
                              W2[m].rearrange("(c p) l -> p c l", p=P)).then_inc(wraw_landed[m], 16)
            act.sem_inc(y_psum_free, 2)
            for s in range(2):
                act.sem_inc(y_stored[s], 16)

            def copy_xT(n, slot):
                act.wait_ge(xT_psum, n + 1)
                nc.scalar.copy(xT_raw[:], ring(slot)).then_inc(xraw_done, 1)

            def round_xT(n, g):
                act.wait_ge(xraw_done, n + 1)
                nc.scalar.copy(xT_hi[:, g % 2], xT_raw[:]).then_inc(xhi_done, 1)

            def gelu(m, k, slot):
                act.wait_ge(s1_done, m + 1)
                nc.scalar.activation(g_raw[:, k % 2], ring(slot), ACT.Gelu,
                                     bias=cols[:, R_B1 + k:R_B1 + k + 1]).then_inc(gelu_done, 1)

            copy_xT(0, 0)
            round_xT(0, 0)
            act.wait_ge(cols_ready, 1)
            act.wait_ge(cond_zeroed, 1)
            nc.scalar.activation(cond_silu[:, :, 0:B], cols[:, R_C:R_C + B * KE].rearrange("p (b k) -> p k b", b=B),
                                 ACT.Silu).then_inc(silu_cond_done, 1)
            nc.scalar.preload_act_table(ACT.Gelu)
            gelu(0, 0, 1)
            gelu(1, 1, 0)

            def stage_y(i, g):
                act.wait_ge(s2_done, K * i + C * g + C)
                act.wait_ge(y_stored[g % 2], 16 * ((G // 2) * i + g // 2 + 1))
                nc.scalar.activation(y_stage[:, g % 2], y_psum(g % 2), ACT.Identity,
                                     bias=cols[:, R_B2 + g:R_B2 + g + 1]).then_inc(y_staged, 1)
                act.wait_ge(y_staged, G * i + g + 1)
                act.sem_inc(y_psum_free, 1)

            def body(i, last):
                slot, _ = PLAN[last]
                for k in range(K):
                    g = k // C
                    if ("T", g + 1) in slot and k % C == 0:
                        act.wait_ge(xlo_done, G * i + g + 1)
                        copy_xT(G * i + g + 1, slot["T", g + 1])
                        round_xT(G * i + g + 1, (g + 1) % G)
                    if ("S", k + 2) in slot:
                        act.wait_ge(glo_done, K * i + k + 1)
                        gelu(K * i + k + 2, (k + 2) % K, slot["S", k + 2])
                    if last and k == K_MEAN:
                        act.wait_ge(y0_stat, 1)
                        nc.scalar.copy(stat[:], ring(slot["M", 0])[:, 0:TB]).then_inc(y0_mean, 1)
                    if last and K_MEAN + 2 <= k < K_MEAN + 6:
                        j = k - K_MEAN - 2
                        act.wait_ge(y0_centred, 2 * j + 2)
                        if j == 0:
                            act.wait_ge(s2_done, K * i + 4 * C)
                        nc.scalar.activation(sq0[:, 2 * j:2 * j + 2], yb0[:, 2 * j:2 * j + 2], ACT.Square
                                             ).then_inc(y0_squared, 1)
                    if last and k == K_VAR:
                        act.wait_ge(y0_stat, 2)
                        act.wait_ge(y0_centred, G)
                        nc.scalar.copy(stat[:], ring(slot["V", 0])[:, 0:TB]).then_inc(y0_var, 1)
                        act.wait_ge(y0_var, 1)
                        nc.scalar.activation(stat[:], stat[:], ACT.Sqrt, bias=eps[:]).then_inc(y0_std, 1)
                        nc.scalar.preload_act_table(ACT.Gelu)
                    if k % C == C - 1 and not (last and g == G - 1):
                        stage_y(i, g)

            with act.Fori(0, NA - 1) as i:
                body(i, False)
            body(NA - 1, True)
            nc.scalar.preload_act_table(ACT.Silu)

            def silu_group(s, b, g):
                return nc.scalar.activation(yb[s][:, g], yb[s][:, g], ACT.Silu,
                                            scale=mod_a[:, b, g:g + 1], bias=mod_c[:, b, g:g + 1])

            act.wait_ge(mod_step, 5)
            for g in range(G):
                if g == HG:
                    stage_y(NA - 1, G - 1)
                act.wait_ge(y0_normed, g + 1)
                silu_group(0, 0, g).then_inc(y0_silu, 1)

            def norm(i, s, b):
                for h in range(2):
                    half = slice(h * HG, (h + 1) * HG)
                    act.wait_ge(centred, 2 * i + h + 1)
                    nc.scalar.activation(sq[:, half], yb[s][:, half], ACT.Square).then_inc(squared, 1)
                nc.scalar.preload_act_table(ACT.Sqrt)
                act.wait_ge(stat_psum, 2 * i + 2)
                nc.scalar.activation(stat[:], var_ps, ACT.Sqrt, bias=eps[:]).then_inc(std_done, 1)
                nc.scalar.preload_act_table(ACT.Silu)
                for g in range(G):
                    if g % HG == 0:
                        act.wait_ge(normed, 2 * i + g // HG + 1)
                    silu_group(s, b, g).then_inc(silu_done, 1)

            with act.Fori(0, NB // 2 - 1) as j:
                norm(2 * j, 1, j)
                norm(2 * j + 1, 0, j + 1)
            norm(NB - 2, 1, NB // 2 - 1)

        @block.vector
        def _(dve):
            nc.vector.memset(stat[:, 0:P], 1.0 / D).then_inc(ones_set, 1)
            nc.vector.memset(eps[:], LN_EPS).then_inc(ones_set, 1)
            nc.vector.memset(cond_silu[:], 0.0).then_inc(cond_zeroed, 1)
            dve.wait_ge(ones_set, 2)
            nc.vector.tensor_copy(ones_r[:], stat[:, 0:P]).then_inc(ones_ready, 1)
            dve.wait_ge(wraw_landed[0], 32)
            for j in range(2):
                raw = wraw[:, 0, j * FF:(j + 1) * FF]
                nc.vector.tensor_copy(W[:, 0, 2 * j], raw).then_inc(w_hi_done, 1)
                dve.wait_ge(w_hi_done, j + 1)
                nc.vector.tensor_tensor(W[:, 0, 2 * j + 1], raw, W[:, 0, 2 * j].bitcast(F32), ALU.subtract
                                        ).then_inc(w_split0, 1)
            dve.wait_ge(vec_turned, 1)
            nc.vector.tensor_copy(cols[:], psum[:, 4, 0:ROWS]).then_inc(cols_ready, 1)

            def rest_xT(n, g):
                dve.wait_ge(xhi_done, n + 1)
                nc.vector.tensor_tensor(xT_lo[:, g % 2], xT_raw[:], xT_hi[:, g % 2].bitcast(F32),
                                        ALU.subtract).then_inc(xlo_done, 1)

            def split_gelu(m, s):
                dve.wait_ge(gelu_done, m + 1)
                nc.vector.tensor_copy(g_hi[:, s], g_raw[:, s]).then_inc(ghi_done, 1)
                dve.wait_ge(ghi_done, m + 1)
                nc.vector.tensor_tensor(g_lo[:, s], g_raw[:, s], g_hi[:, s].bitcast(F32),
                                        ALU.subtract).then_inc(glo_done, 1)

            def modulation():
                dve.wait_ge(emb_copied, KE + 1)
                nc.vector.tensor_tensor(emb[:], emb[:], cols[:, R_EB:R_EB + NE].unsqueeze(2).to_broadcast([P, NE, B]),
                                        ALU.add).then_inc(mod_step, 1)
                dve.wait_ge(mod_step, 1)
                scale = emb[:, 0:G].rearrange("p g b -> p b g")
                shift = emb[:, G:NE].rearrange("p g b -> p b g")
                g_all = cols[:, R_G:R_G + G].unsqueeze(1).to_broadcast([P, B, G])
                b_all = cols[:, R_B:R_B + G].unsqueeze(1).to_broadcast([P, B, G])
                nc.vector.tensor_scalar(mod_t[:], scale, 1.0, None, ALU.add).then_inc(mod_step, 1)
                dve.wait_ge(mod_step, 2)
                nc.vector.tensor_tensor(mod_a[:], mod_t[:], g_all, ALU.mult).then_inc(mod_step, 1)
                nc.vector.tensor_tensor(mod_c[:], mod_t[:], b_all, ALU.mult).then_inc(mod_step, 1)
                dve.wait_ge(mod_step, 4)
                nc.vector.tensor_tensor(mod_c[:], mod_c[:], shift, ALU.add).then_inc(mod_step, 1)

            rest_xT(0, 0)
            split_gelu(0, 0)
            split_gelu(1, 1)

            def body(i, last):
                slot, _ = PLAN[last]
                for k in range(K):
                    g = k // C
                    if last and k in K_EMB:
                        r = K_EMB.index(k)
                        dve.wait_ge(emb_chunk, r + 1)
                        ps = ring(slot["E", r])[:, 0:BANK]
                        if r == 0:
                            nc.vector.tensor_copy(emb_rows[:], ps).then_inc(emb_copied, 1)
                        else:
                            dve.wait_ge(emb_copied, r)
                            nc.vector.tensor_tensor(emb_rows[:], ps, emb_rows[:], ALU.add).then_inc(emb_copied, 1)
                    if last and k == K_TURN:
                        dve.wait_ge(emb_turned, 1)
                        ps = ring(slot["F", 0])[:, 0:BANK].rearrange("p (c j m) -> p j c m", c=4, j=4)
                        nc.vector.tensor_copy(emb[:].rearrange("p (j c) b -> p j c b", j=4), ps[:, :, :, 0:B]
                                              ).then_inc(emb_copied, 1)
                    if ("T", g + 1) in slot and k % C == 0:
                        rest_xT(G * i + g + 1, (g + 1) % G)
                    if ("S", k + 2) in slot:
                        dve.wait_ge(s2_done, K * i + k + 1)
                        split_gelu(K * i + k + 2, k % 2)
                    if last and k in (K_VAR + 1, K_VAR + 2, K_VAR + 3):
                        dve.wait_ge(y0_std, 1)
                        cuts = (0, 160, 336, TB)
                        piece = slice(cuts[k - K_VAR - 1], cuts[k - K_VAR])
                        nc.vector.reciprocal(stat[:, piece], stat[:, piece]).then_inc(y0_rstd, 1)
                    if last and k == K_TURN + 2:
                        modulation()

            with dve.Fori(0, NA - 1) as i:
                body(i, False)
            body(NA - 1, True)

            for h in range(HG):
                two = slice(2 * h, 2 * h + 2)
                dve.wait_ge(y0_silu, 2 * h + 2)
                nc.vector.tensor_copy(s_hi0[:, two], yb0[:, two]).then_inc(y0_shi, 1)
                dve.wait_ge(y0_shi, h + 1)
                nc.vector.tensor_tensor(s_lo0[:, two], yb0[:, two], s_hi0[:, two].bitcast(F32),
                                        ALU.subtract).then_inc(y0_slo, 1)

            def group_sum(n, src):
                nc.vector.tensor_tensor(sq[:, 0:4], src[:, 0:4], src[:, 4:8], ALU.add).then_inc(tree, 1)
                dve.wait_ge(tree, 3 * n + 1)
                nc.vector.tensor_tensor(sq[:, 0:2], sq[:, 0:2], sq[:, 2:4], ALU.add).then_inc(tree, 1)
                dve.wait_ge(tree, 3 * n + 2)
                nc.vector.tensor_tensor(stat[:], sq[:, 0], sq[:, 1], ALU.add).then_inc(tree, 1)
                dve.wait_ge(tree, 3 * n + 3)
                nc.vector.tensor_copy(sum_hi[:], stat[:]).then_inc(sum_split, 1)
                dve.wait_ge(sum_split, 2 * n + 1)
                nc.vector.tensor_tensor(sum_lo[:], stat[:], sum_hi[:].bitcast(F32), ALU.subtract
                                        ).then_inc(sum_split, 1)

            def finish(i, t):
                dve.wait_ge(proj_done, SB * i + t + 1)
                dve.wait_ge(res_biased, SB * i + t + 1)
                nc.vector.tensor_tensor(res[:, t % 2], proj[t % 2], res[:, t % 2], ALU.add
                                        ).then_inc(out_ready, 1)

            def centre(i, s, h):
                half = yb[s][:, h * HG:(h + 1) * HG]
                nc.vector.tensor_tensor(half, half, mean_ps.unsqueeze(1).to_broadcast([P, HG, TB]),
                                        ALU.subtract).then_inc(centred, 1)

            def normalise(i, s, h):
                half = yb[s][:, h * HG:(h + 1) * HG]
                nc.vector.tensor_tensor(half, half, stat[:].unsqueeze(1).to_broadcast([P, HG, TB]),
                                        ALU.mult).then_inc(normed, 1)

            def split_silu(i, s, h):
                half = slice(h * HG, (h + 1) * HG)
                dve.wait_ge(silu_done, G * i + (h + 1) * HG)
                nc.vector.tensor_copy(s_hi[s][:, half], yb[s][:, half]).then_inc(shi_done, 1)
                dve.wait_ge(shi_done, 2 * i + h + 1)
                nc.vector.tensor_tensor(s_lo[s][:, half], yb[s][:, half], s_hi[s][:, half].bitcast(F32),
                                        ALU.subtract).then_inc(slo_done, 1)

            def window(i, s, landed, last):
                if last:
                    for t in range(SB):
                        finish(i, t)
                    return
                dve.wait_ge(y_landed[s], 16 * landed)
                group_sum(2 * i, yb[s])
                dve.wait_ge(stat_psum, 2 * i + 1)
                centre(i, s, 0)
                centre(i, s, 1)
                finish(i, 0)
                dve.wait_ge(squared, 2 * i + 2)
                group_sum(2 * i + 1, sq)
                dve.wait_ge(std_done, i + 1)
                nc.vector.reciprocal(stat[:], stat[:]).then_inc(rstd_done, 1)
                finish(i, 1)
                dve.wait_ge(rstd_done, i + 1)
                normalise(i, s, 0)
                normalise(i, s, 1)
                split_silu(i, s, 0)
                finish(i, 2)
                split_silu(i, s, 1)
                finish(i, 3)

            dve.wait_ge(s2_done, K * NA)
            with dve.Fori(0, NB // 2 - 1) as j:
                window(2 * j, 1, j + 1, False)
                window(2 * j + 1, 0, j + 1, False)
            window(NB - 2, 1, NB // 2, False)
            window(NB - 1, 0, 0, True)

        @block.tensor
        def _(pe):
            def turn_x(slot, g):
                for s in range(SUB):
                    mm = nc.tensor.transpose(ring(slot)[:, s * P:(s + 1) * P], xin[:, g % 2, s], ident[:])
                mm.then_inc(xT_psum, 1)

            def first(k, slot):
                g, c = k // C, k % C
                cut = slice(c * P, (c + 1) * P)
                for n, (w, v) in enumerate(((W1_HI, xT_hi), (W1_LO, xT_hi), (W1_HI, xT_lo))):
                    for h in range(2):
                        mm = nc.tensor.matmul(ring(slot)[:, h * BANK:(h + 1) * BANK], W[:, g, w, cut],
                                              v[:, g % 2, h * BANK:(h + 1) * BANK],
                                              start=(n == 0), stop=(n == 2))
                mm.then_inc(s1_done, 1)

            def second(k):
                g, c = k // C, k % C
                cut = slice(c * P, (c + 1) * P)
                for n, (w, v) in enumerate(((W2_HI, g_hi), (W2_LO, g_hi), (W2_HI, g_lo))):
                    for h in range(2):
                        mm = nc.tensor.matmul(y_psum(g % 2)[:, h * BANK:(h + 1) * BANK], W[:, g, w, cut],
                                              v[:, k % 2, h * BANK:(h + 1) * BANK],
                                              start=(c == 0 and n == 0), stop=(c == C - 1 and n == 2))
                mm.then_inc(s2_done, 1)

            def mean_of_sum(ps):
                nc.tensor.matmul(ps, ones_r[:], sum_hi[:], start=True, stop=False)
                return nc.tensor.matmul(ps, ones_r[:], sum_lo[:], start=False, stop=True)

            def embed(r, ps):
                pe.wait_ge(emb_landed, 16 * (r + 1))
                for j in range(4):
                    mm = nc.tensor.matmul(ps[32 * j:32 * j + 32, 0:BANK], cond_silu[:, r],
                                          wraw[:].rearrange("p s q -> p (s q)")[:, j * BANK:(j + 1) * BANK],
                                          start=True, stop=True, tile_position=(0, 32 * j))
                mm.then_inc(emb_chunk, 1)

            pe.wait_ge(ident_ready, 1)
            pe.wait_ge(x_landed[0], 16)
            turn_x(0, 0)
            pe.wait_ge(vec_landed, 16 * 6)
            nc.tensor.transpose(psum[:, 4, 0:ROWS], vec_rows[0:ROWS, :], ident[0:ROWS, 0:ROWS]
                                ).then_inc(vec_turned, 1)
            pe.wait_ge(w_split0, 2)
            pe.wait_ge(xlo_done, 1)
            first(0, 1)
            first(1, 0)

            def body(i, last):
                slot, before = PLAN[last]

                def take(use):
                    kind, n = before[use]
                    if kind == "S":
                        pe.wait_ge(gelu_done, K * i + n + 1)
                    elif kind == "T":
                        pe.wait_ge(xraw_done, G * i + n + 1)
                    elif kind == "E":
                        pe.wait_ge(emb_copied, n + 1)
                    elif kind == "F":
                        pe.wait_ge(emb_copied, KE + 1)
                    else:
                        pe.wait_ge({"M": y0_mean, "V": y0_var}[kind], 1)
                    return slot[use]

                for k in range(K):
                    g = k // C
                    if k % C == 0 and ("T", g + 1) in slot:
                        if g + 1 < G:
                            pe.wait_ge(x_landed[(g + 1) % 2], 16 * ((G // 2) * i + (g + 1) // 2 + 1))
                        else:
                            pe.wait_ge(x_landed[0], 16 * ((G // 2) * i + G // 2 + 1))
                        turn_x(take(("T", g + 1)), (g + 1) % G)
                    if last and k in K_EMB:
                        r = K_EMB.index(k)
                        embed(r, ring(take(("E", r))))
                    if last and k == K_TURN:
                        ps = ring(take(("F", 0)))
                        pe.wait_ge(emb_copied, KE)
                        for c in range(4):
                            mm = nc.tensor.transpose(ps[:, c * P:(c + 1) * P], emb_rows[:, c * P:(c + 1) * P],
                                                     ident[:])
                        mm.then_inc(emb_turned, 1)
                    if last and k == K_MEAN:
                        s = take(("M", 0))
                        pe.wait_ge(y0_split, 2)
                        mean_of_sum(ring(s)[:, 0:TB]).then_inc(y0_stat, 1)
                    if last and k == K_VAR:
                        s = take(("V", 0))
                        pe.wait_ge(y0_split, 4)
                        mean_of_sum(ring(s)[:, 0:TB]).then_inc(y0_stat, 1)
                    if ("S", k + 2) in slot:
                        s = take(("S", k + 2))
                        if k % C == C - 2:
                            pe.wait_ge(xlo_done, G * i + g + 2)
                            if g + 1 < G:
                                pe.wait_ge(pw_split, 2 * (g + 1))
                        first((k + 2) % K, s)
                    pe.wait_ge(glo_done, K * i + k + 1)
                    if k % C == 0:
                        pe.wait_ge(y_psum_free, G * i + g + 1)
                    second(k)

            pe.wait_ge(silu_cond_done, 1)
            pe.wait_ge(ones_ready, 1)
            with pe.Fori(0, NA - 1) as i:
                body(i, False)
            body(NA - 1, True)

            def project(s, t, g):
                cut = slice(t * P, (t + 1) * P)
                for n, (v, w) in enumerate(((s_hi[s], oW_hi), (s_hi[s], oW_lo), (s_lo[s], oW_hi))):
                    for h in range(2):
                        mm = nc.tensor.matmul(proj[t % 2][:, h * BANK:(h + 1) * BANK], v[:, g, cut],
                                              w[:, g, h * BANK:(h + 1) * BANK],
                                              start=(g == 0 and n == 0), stop=(g == G - 1 and n == 2))
                if g == G - 1:
                    mm.then_inc(proj_done, 1)

            def window(i, s, first, last):
                at_mean, at_var = ((1, 1), (2, 4)) if first else ((1, 0), (2, 2))
                for t in range(SB):
                    if not (first and t < 2):
                        pe.wait_ge(out_ready, SB * i + t - 1)
                    for g in range(G):
                        if t == 0 and first and g % 2 == 0:
                            pe.wait_ge(y0_slo, g // 2 + 1)
                        if t == 0 and not first and g % HG == 0:
                            pe.wait_ge(slo_done, 2 * i - 2 + g // HG + 1)
                        project(s, t, g)
                        if (t, g) == at_mean and not last:
                            if first:
                                pe.wait_ge(y_psum_free, NA * G + 2)
                            pe.wait_ge(sum_split, 4 * i + 2)
                            mean_of_sum(mean_ps).then_inc(stat_psum, 1)
                        if (t, g) == at_var and not last:
                            pe.wait_ge(sum_split, 4 * i + 4)
                            mean_of_sum(var_ps).then_inc(stat_psum, 1)

            window(0, 0, True, False)
            window(1, 1, False, False)
            with pe.Fori(1, NB // 2 - 1) as j:
                window(2 * j, 0, False, False)
                window(2 * j + 1, 1, False, False)
            window(NB - 2, 0, False, False)
            window(NB - 1, 1, False, True)


_INS = ["x", "cond_2048", "L0_cond_W1", "L0_cond_b1", "L0_cond_W2", "L0_cond_b2", "L0_cond_emb_W",
        "L0_cond_emb_b", "L0_cond_ln_g", "L0_cond_ln_b", "L0_cond_out_W", "L0_cond_out_b"]


def kernel(**inputs):
    import numpy as _np
    import concourse.bacc as _bacc
    from concourse import mybir as _mybir
    from concourse.bass_utils import run_bass_kernel_spmd as _run

    nc = _bacc.Bacc("TRN2", target_bir_lowering=False, num_devices=1)
    arrays, args = {}, []
    for name in _INS:
        a = _np.ascontiguousarray(inputs[name])
        arrays[f"in_{name}"] = a
        args.append(nc.dram_tensor(f"in_{name}", a.shape, _mybir.dt.from_np(a.dtype), kind="ExternalInput").ap())
    args.append(nc.dram_tensor("out", arrays["in_x"].shape, F32, kind="ExternalOutput").ap())
    cond_ffn_program(nc, *args)
    r = _run(nc, [arrays], core_ids=[0])
    return r.results[0]["out"]
```

```python
from contextlib import ExitStack

import concourse.bass as bass
from concourse import mybir

P = 128
F32 = mybir.dt.float32
F32R = mybir.dt.float32r
ALU = mybir.AluOpType
ACT = mybir.ActivationFunctionType

BANK = 512
LN_EPS = 1e-5


def cond_ffn_program(nc, x, cond, W1, b1, W2, b2, emb_W, emb_b, ln_g, ln_b, out_W, out_b, out):
    B, T, D = x.shape
    G, L, FF = W1.shape
    C = FF // P
    KE = cond.shape[1] // P
    NE = emb_W.shape[1] // P
    TA = T
    SUB = TA // P
    NA = B * T // TA
    TB = BANK
    H = TA // TB
    NB = B * T // TB
    SB = TB // P
    K = G * C
    assert L == P and D == G * L and TA == 2 * BANK and D == 2 * BANK and G % 2 == 0 and C == 4

    y_scratch = nc.dram_tensor("y_scratch", [NB, P, G, TB], F32, kind="Internal").ap()

    R_B1 = 0
    R_B2 = R_B1 + G * C
    R_EB = R_B2 + G
    R_G = R_EB + NE
    R_B = R_G + G
    R_C = R_B + G
    ROWS = R_C + B * KE
    assert ROWS <= P

    with ExitStack() as ctx:
        def sb(name, shape, dt=F32, scope=ctx):
            return scope.enter_context(nc.sbuf_tensor(name, shape, dt))

        def sem(name):
            return ctx.enter_context(nc.semaphore(name))

        psum = ctx.enter_context(nc.psum_tensor("psum", [P, 8, BANK], F32))

        oW_hi = sb("oW_hi", [P, G, D], F32R)
        oW_lo = sb("oW_lo", [P, G, D], F32R)
        ident = sb("ident", [P, P])
        cols = sb("cols", [P, ROWS])
        ones_r = sb("ones_r", [P, P], F32R)
        eps = sb("eps", [P, 1])
        stat = sb("stat", [P, TB])
        sum_hi = sb("sum_hi", [P, TB], F32R)
        sum_lo = sb("sum_lo", [P, TB], F32R)
        cond_silu = sb("cond_silu", [P, KE, 32])
        cond_now = sb("cond_now", [P, 2, 32])
        emb_rows = sb("emb_rows", [P, BANK])
        sq_sum = emb_rows
        vec_rows = emb_rows[:, 0:P]
        emb = sb("emb", [P, NE, B])
        mod_a = sb("mod_a", [P, B, G])
        mod_c = sb("mod_c", [P, B, G])
        mod_t = sb("mod_t", [P, B, G])

        with ExitStack() as a:
            W = sb("W", [P, G, 4, FF], F32R, a)
            xT_hi = sb("xT_hi", [P, 2, TA], F32R, a)
            xT_lo = sb("xT_lo", [P, 2, TA], F32R, a)
            g_raw = sb("g_raw", [P, 2, TA], F32, a)
            g_hi = sb("g_hi", [P, 2, TA], F32R, a)
            g_lo = sb("g_lo", [P, 2, TA], F32R, a)
            xT_raw = sb("xT_raw", [P, TA], F32, a)
            xin = sb("xin", [P, 2, SUB, P], F32, a)
            y_stage = sb("y_stage", [P, 2, TA], F32, a)
            wraw = sb("wraw", [P, 2, 2 * FF], F32, a)
            assert D == 2 * FF == KE * P

        with ExitStack() as b:
            yb0 = sb("yb0", [P, G, TB], F32, b)
            s_lo0 = sb("s_lo0", [P, G, TB], F32R, b)
            s_hi0 = sb("s_hi0", [P, G, TB], F32R, b)
            sq = sb("sq", [P, G, TB], F32, b)
            yb1 = sb("yb1", [P, G, TB], F32, b)
            s_hi1 = sb("s_hi1", [P, G, TB], F32R, b)
            s_lo1 = sb("s_lo1", [P, G, TB], F32R, b)
            res = sb("res", [P, 2, D], F32, b)
            out_b_all = sb("out_b_all", [P, D], F32, b)
        yb = (yb0, yb1)
        s_hi = (s_hi0, s_hi1)
        s_lo = (s_lo0, s_lo1)
        W1_HI, W1_LO, W2_HI, W2_LO = range(4)
        HG = G // 2
        squares = wraw[:].rearrange("p s (g t) -> p (s g) t", g=2)

        sp_waits = sem("sp_waits")

        ident_zeroed = sem("ident_zeroed")
        ident_ready = sem("ident_ready")
        vec_landed = sem("vec_landed")
        vec_landed_pool = sem("vec_landed_pool")
        vec_turned = sem("vec_turned")
        cols_ready = sem("cols_ready")
        ones_set = sem("ones_set")
        ones_ready = sem("ones_ready")
        wraw_landed = [sem(f"wraw_landed{s}") for s in range(2)]
        w1_landed = sem("w1_landed")
        w_hi_done = sem("w_hi_done")
        w_split0 = sem("w_split0")
        aw_hi_done = sem("aw_hi_done")
        pw_split = sem("pw_split")
        silu_cond_done = sem("silu_cond_done")
        cond_zeroed = sem("cond_zeroed")
        emb_landed = sem("emb_landed")
        cond_now_ready = sem("cond_now_ready")
        emb_chunk = sem("emb_chunk")
        emb_copied = sem("emb_copied")
        emb_turned = sem("emb_turned")
        mod_step = sem("mod_step")

        x_landed = [sem(f"x_landed{s}") for s in range(2)]
        x0_landed = [sem(f"x0_landed{h}") for h in range(2)]
        x0T_psum = sem("x0T_psum")
        x0_raw = sem("x0_raw")
        x0_hi = sem("x0_hi")
        x0_lo = sem("x0_lo")
        xT_psum = sem("xT_psum")
        xraw_done = sem("xraw_done")
        xhi_done = sem("xhi_done")
        xlo_done = sem("xlo_done")
        s1_done = sem("s1_done")
        gelu_done = sem("gelu_done")
        ghi_done = sem("ghi_done")
        glo_done = sem("glo_done")
        s2_done = sem("s2_done")
        y_psum_free = sem("y_psum_free")
        y_staged = sem("y_staged")
        y_stored = [sem(f"y_stored{s}") for s in range(2)]

        y0_landed = sem("y0_landed")
        y0_sum = sem("y0_sum")
        y0_split = sem("y0_split")
        y0_stat = sem("y0_stat")
        y0_mean = sem("y0_mean")
        y0_centred = sem("y0_centred")
        y0_squared = sem("y0_squared")
        y0_var = sem("y0_var")
        y0_std = sem("y0_std")
        y0_rstd = sem("y0_rstd")
        y0_normed = sem("y0_normed")
        y0_silu = sem("y0_silu")
        y0_shi = sem("y0_shi")
        y0_slo = sem("y0_slo")

        y_landed = [sem(f"y_landed{s}") for s in range(2)]
        tree = sem("tree")
        sum_split = sem("sum_split")
        stat_psum = sem("stat_psum")
        centred = sem("centred")
        squared = sem("squared")
        std_done = sem("std_done")
        rstd_done = sem("rstd_done")
        normed = sem("normed")
        silu_done = sem("silu_done")
        shi_done = sem("shi_done")
        slo_done = sem("slo_done")
        proj_done = sem("proj_done")
        out_b_landed = sem("out_b_landed")
        res_landed = [sem(f"res_landed{s}") for s in range(2)]
        res_biased = sem("res_biased")
        out_ready = sem("out_ready")
        out_stored = [sem(f"out_stored{s}") for s in range(2)]

        def ring(s):
            return psum[:, 2 * s:2 * s + 2, :].rearrange("p b n -> p (b n)")

        def y_psum(s):
            return psum[:, 4 + 2 * s:6 + 2 * s, :].rearrange("p b n -> p (b n)")

        proj = [ring(0), ring(1)]
        mean_ps = psum[:, 4]
        var_ps = psum[:, 5]

        PERIOD = 16
        AT_ROUND = (2, 5)
        AT_LOAD = (6, 10)
        AT_EMB = (10, 14)
        K_EMB = [p + k for p in range(0, K, PERIOD) for k in AT_EMB]
        E_PER_BLOCK = len(K_EMB)
        K_TURN = 2
        K_MEAN, K_Y0, K_SQ, K_VAR, K_INV = 3, (4, 8), (7, 9, 13, 14), 18, (19, 21, 22)
        Y0_PARTS = [slice(0, 1), slice(1, 2)] + [slice(g, g + 2) for g in range(2, G, 2)]
        assert E_PER_BLOCK * (NA - 2) == KE and NE == 4 * BANK // P
        FIRST, MIDDLE, LAST = range(3)

        def ring_plan(kind):
            last = kind == LAST
            uses = [("S", 0), ("S", 1)]
            for k in range(K):
                if k % C == 0 and not (last and k // C + 1 == G):
                    uses.append(("T", k // C + 1))
                if kind == MIDDLE and k in K_EMB:
                    uses.append(("E", K_EMB.index(k)))
                if last and k == K_TURN:
                    uses.append(("F", 0))
                if last and k == K_MEAN:
                    uses.append(("M", 0))
                if last and k == K_VAR:
                    uses.append(("V", 0))
                if not (last and k + 2 >= K):
                    uses.append(("S", k + 2))
            slot = {u: (j + 1) % 2 for j, u in enumerate(uses)}
            before = {u: uses[j - 2] for j, u in enumerate(uses) if j >= 2}
            return slot, before

        PLAN = [ring_plan(kind) for kind in (FIRST, MIDDLE, LAST)]

        x_cols = x.rearrange("b (s p) (g l) -> b g p s l", p=P, l=L)
        y_out = y_scratch.rearrange("(i h) p g t -> i g p h t", h=H)
        oW_rows = out_W.rearrange("(g p) n -> g p n", p=P)
        emb_rows_in = emb_W.rearrange("(r p) n -> r p n", p=P)
        PERIODS = K // PERIOD
        assert 2 * PERIODS * (NA - 2) == G

        def load_weights(engine, m):
            s = m % 2
            engine.dma_start(wraw[:, s, 0:FF], W1[m]).then_inc(w1_landed if m == 0 else wraw_landed[s], 16)
            engine.dma_start(wraw[:, s, FF:2 * FF].rearrange("p (c l) -> p c l", c=C),
                             W2[m].rearrange("(c p) l -> p c l", p=P)).then_inc(wraw_landed[s], 16)

        def landed(m):
            return 32 * (m // 2 + 1) - (16 if m % 2 == 0 else 0)

        x_rows = x.rearrange("b (h s p) d -> (b h) s p d", p=P, s=SB)
        out_rows = out.rearrange("b (h s p) d -> (b h) s p d", p=P, s=SB)

        small_vectors = ((R_B1, b1.rearrange("g (c p) -> (g c) p", p=P)), (R_B2, b2),
                         (R_C, cond.rearrange("b (k p) -> (b k) p", p=P)),
                         (R_EB, emb_b.rearrange("(n p) -> n p", p=P)),
                         (R_G, ln_g.rearrange("(n p) -> n p", p=P)),
                         (R_B, ln_b.rearrange("(n p) -> n p", p=P)))

        block = ctx.enter_context(nc.Block())

        @block.sync
        def _(sp):
            def wait(signal, value):
                sp.wait_ge(signal, value)
                sp.sem_inc(sp_waits, 1)

            def load_x(i, g):
                sp.dma_start(xin[:, g % 2], x_cols[i, g]).then_inc(x_landed[g % 2], 16)

            for h in range(2):
                part = slice(h * SB, (h + 1) * SB)
                sp.dma_start(xin[:, 0, part], x_cols[0, 0, :, part]).then_inc(x0_landed[h], 16)
            for r0, v in small_vectors[:3]:
                sp.dma_start(vec_rows[r0:r0 + v.shape[0], :], v).then_inc(vec_landed, 16)
            load_x(0, 1)
            load_weights(sp, 1)

            def load_emb(r):
                sp.dma_start(wraw[:].rearrange("p s q -> p (s q)"), emb_rows_in[r]
                             ).then_inc(emb_landed, 16)

            def body(i, kind):
                start, last = kind == FIRST, kind == LAST
                for k in range(K):
                    g = k // C
                    if start and k % C == 0 and g + 2 < G:
                        if g == 0:
                            wait(w_split0, 2)
                        else:
                            wait(pw_split, 2 * g)
                        load_weights(sp, g + 2)
                    if kind == MIDDLE:
                        p = PERIODS * i - PERIODS + k // PERIOD
                        if k % PERIOD == 0:
                            wait(pw_split, 2 * (G - 1) + 4 * p)
                            wait(emb_chunk, 2 * p + 1)
                            for s in range(2):
                                sp.dma_start(wraw[:, s], oW_rows[2 * p + s]).then_inc(wraw_landed[s], 16)
                        if k % PERIOD == AT_LOAD[0]:
                            wait(pw_split, 2 * (G - 1) + 4 * p + 4)
                            load_emb(2 * p)
                        if k % PERIOD == AT_LOAD[1]:
                            wait(emb_chunk, 2 * p + 2)
                            load_emb(2 * p + 1)
                    if k % C == 0 and not (last and g + 2 >= G):
                        wait(xT_psum, G * i + g + 1)
                        if g + 2 < G:
                            load_x(i, g + 2)
                        else:
                            load_x(i + 1, g + 2 - G)
                    if last and k in K_Y0:
                        h = K_Y0.index(k)
                        half = slice(h * HG, (h + 1) * HG)
                        wait(s2_done, K * i + (h + 1) * C)
                        for s in range(2):
                            wait(y_stored[s], 16 * (G // 2 + 1))
                        sp.dma_start(yb[0][:, half], y_scratch[0, :, half]).then_inc(y0_landed, 16)
                    if last and k == K - 2:
                        wait(s1_done, K * NA)
                        sp.dma_start(yb[1][:], y_scratch[1]).then_inc(y_landed[1], 16)
                    if k % C == C - 1:
                        wait(y_staged, G * i + g + 1)
                        sp.dma_start(y_out[i, g], y_stage[:, g % 2].rearrange("p (h t) -> p h t", h=H)
                                     ).then_inc(y_stored[g % 2], 16)

            body(0, FIRST)
            with sp.Fori(1, NA - 1) as i:
                body(i, MIDDLE)
            body(NA - 1, LAST)
            for s in range(2):
                wait(y_stored[s], 16 * (NA * G // 2 + 1))

            def load_res(i, t):
                sp.dma_start(res[:, t % 2], x_rows[i, t]).then_inc(res_landed[t % 2], 16)

            sp.dma_start(out_b_all[:], out_b.rearrange("(o d) -> o d", o=1).to_broadcast([P, D])
                         ).then_inc(out_b_landed, 16)
            load_res(0, 0)
            load_res(0, 1)
            wait(y0_slo, len(Y0_PARTS))
            sp.dma_start(yb[0][:], y_scratch[2]).then_inc(y_landed[0], 16)

            def window(i, w, load, last):
                for t in range(SB - 1 if last else SB):
                    wait(out_ready, SB * i + t + 1)
                    sp.dma_start(out_rows[i, t], res[:, t % 2]).then_inc(out_stored[t % 2], 16)
                    if not (last and t + 2 >= SB):
                        wait(out_stored[t % 2], 16 * ((SB // 2) * i + t // 2 + 1))
                        load_res(i + (t + 2) // SB, (t + 2) % SB)
                if last:
                    for h in range(2):
                        part = slice(h * BANK, (h + 1) * BANK)
                        wait(out_ready, SB * NB + h)
                        sp.dma_start(out_rows[i, SB - 1, :, part], res[:, 1, part]).then_inc(out_stored[1], 16)
                if load:
                    s = (w + 1) % 2
                    wait(slo_done, 2 * i + 2)
                    sp.dma_start(yb[s][:], y_scratch[i + 3]).then_inc(y_landed[s], 16)

            with sp.Fori(0, NB // 2 - 2) as j:
                window(2 * j, 0, True, False)
                window(2 * j + 1, 1, True, False)
            for i in range(NB - 4, NB):
                window(i, i % 2, i + 3 < NB, i == NB - 1)
            for s in range(2):
                wait(out_stored[s], 16 * (NB * SB // 2 + s))

        @block.gpsimd
        def _(pool):
            nc.gpsimd.memset(ident[:], 0.0).then_inc(ident_zeroed, 1)
            pool.wait_ge(ident_zeroed, 1)
            nc.gpsimd.affine_select(out=ident[:], in_=ident[:], compare_op=ALU.not_equal, fill=1.0,
                                    base=0, pattern=[[-1, P]], channel_multiplier=1).then_inc(ident_ready, 1)
            for r0, v in small_vectors[3:]:
                pool.dma_start(vec_rows[r0:r0 + v.shape[0], :], v).then_inc(vec_landed_pool, 16)

            def low(hi, lo, raw):
                nc.gpsimd.tensor_tensor(lo, raw, hi.bitcast(F32), ALU.subtract).then_inc(pw_split, 1)

            def split_sum(total, n):
                nc.gpsimd.tensor_copy(sum_hi[:], total[:]).then_inc(y0_split, 1)
                pool.wait_ge(y0_split, 2 * n + 1)
                nc.gpsimd.tensor_tensor(sum_lo[:], total[:], sum_hi[:].bitcast(F32), ALU.subtract
                                        ).then_inc(y0_split, 1)

            pool.wait_ge(ones_ready, 1)
            for m in range(1, G + 2):
                if m >= 2:
                    g = m - 2
                    pool.wait_ge(y_staged, g + 1)
                    if g == 0:
                        nc.gpsimd.tensor_copy(stat[:], y_stage[:, 0, 0:TB]).then_inc(y0_sum, 1)
                    else:
                        pool.wait_ge(y0_sum, g)
                        nc.gpsimd.tensor_tensor(stat[:], stat[:], y_stage[:, g % 2, 0:TB], ALU.add
                                                ).then_inc(y0_sum, 1)
                if m >= G:
                    continue
                pool.wait_ge(wraw_landed[m % 2], landed(m))
                for j in range(2):
                    pool.wait_ge(aw_hi_done, 2 * (m - 1) + j + 1)
                    low(W[:, m, 2 * j], W[:, m, 2 * j + 1], wraw[:, m % 2, j * FF:(j + 1) * FF])
            pool.wait_ge(y0_sum, G)
            split_sum(stat, 0)
            with pool.Fori(0, G // 2) as j:
                for s in range(2):
                    pool.wait_ge(aw_hi_done, 2 * (G - 1) + 2 * j + s + 1)
                    for c in (0, FF):
                        low(oW_hi[:, 2 * j + s, c:c + FF], oW_lo[:, 2 * j + s, c:c + FF], wraw[:, s, c:c + FF])
                pool.wait_ge(silu_cond_done, 1)
                pool.wait_ge(emb_chunk, 2 * j + 1)
                nc.gpsimd.tensor_copy(cond_now[:], cond_silu[:, bass.ds(2 * j, 2)]).then_inc(cond_now_ready, 1)

            pool.wait_ge(emb_turned, 1)
            pool.wait_ge(y0_mean, 1)
            for h in range(2):
                pool.wait_ge(y0_landed, 16 * (h + 1))
                for g in range(h * HG, (h + 1) * HG):
                    nc.gpsimd.tensor_tensor(yb0[:, g], yb0[:, g], stat[:], ALU.subtract).then_inc(y0_centred, 1)
                for g in range(max(h * HG, 1), (h + 1) * HG):
                    pool.wait_ge(y0_squared, g // 2 + 1)
                    if g > 1:
                        pool.wait_ge(y0_sum, G + g - 1)
                    nc.gpsimd.tensor_tensor(sq_sum[:], squares[:, 0] if g == 1 else sq_sum[:], squares[:, g % HG],
                                            ALU.add).then_inc(y0_sum, 1)
            pool.wait_ge(y0_sum, 2 * G - 1)
            pool.wait_ge(y0_stat, 1)
            split_sum(sq_sum, 1)
            pool.wait_ge(y0_rstd, 3)
            for g in range(G):
                nc.gpsimd.tensor_tensor(yb0[:, g], yb0[:, g], stat[:], ALU.mult).then_inc(y0_normed, 1)

            pool.wait_ge(out_b_landed, 16)
            with pool.Fori(0, NB) as i:
                for t in range(SB):
                    pool.wait_ge(res_landed[t % 2], 16 * ((SB // 2) * i + t // 2 + 1))
                    nc.gpsimd.tensor_tensor(res[:, t % 2], res[:, t % 2], out_b_all[:], ALU.add
                                            ).then_inc(res_biased, 1)

        @block.scalar
        def _(act):
            load_weights(act, 0)
            nc.scalar.preload_act_table(ACT.Silu)
            act.sem_inc(y_psum_free, 2)
            for s in range(2):
                act.sem_inc(y_stored[s], 16)
            act.sem_inc(emb_chunk, 1)

            def copy_xT(n, slot):
                act.wait_ge(xT_psum, n + 1)
                nc.scalar.copy(xT_raw[:], ring(slot)).then_inc(xraw_done, 1)

            def round_xT(n, g):
                act.wait_ge(xraw_done, n + 1)
                nc.scalar.copy(xT_hi[:, g % 2], xT_raw[:]).then_inc(xhi_done, 1)

            def gelu(m, k, slot):
                act.wait_ge(s1_done, m + 1)
                nc.scalar.activation(g_raw[:, k % 2], ring(slot), ACT.Gelu,
                                     bias=cols[:, R_B1 + k:R_B1 + k + 1]).then_inc(gelu_done, 1)

            for h in range(2):
                part = slice(h * BANK, (h + 1) * BANK)
                if h == 0:
                    act.wait_ge(x0T_psum, 1)
                else:
                    act.wait_ge(xT_psum, 1)
                nc.scalar.copy(xT_raw[:, part], ring(0)[:, part]).then_inc(xraw_done if h else x0_raw, 1)
                act.wait_ge(xraw_done if h else x0_raw, 1)
                nc.scalar.copy(xT_hi[:, 0, part], xT_raw[:, part]).then_inc(xhi_done if h else x0_hi, 1)
            act.wait_ge(cols_ready, 1)
            act.wait_ge(cond_zeroed, 1)
            nc.scalar.activation(cond_silu[:, :, 0:B], cols[:, R_C:R_C + B * KE].rearrange("p (b k) -> p k b", b=B),
                                 ACT.Silu).then_inc(silu_cond_done, 1)
            nc.scalar.preload_act_table(ACT.Gelu)
            gelu(0, 0, 1)
            gelu(1, 1, 0)

            def round_group(m):
                act.wait_ge(wraw_landed[m % 2], landed(m))
                for j in range(2):
                    nc.scalar.copy(W[:, m, 2 * j], wraw[:, m % 2, j * FF:(j + 1) * FF]).then_inc(aw_hi_done, 1)

            round_group(1)

            def stage_y(i, g, add_up=None):
                act.wait_ge(s2_done, K * i + C * g + C)
                act.wait_ge(y_stored[g % 2], 16 * ((G // 2) * i + g // 2 + 1))
                if add_up is not None:
                    act.wait_ge(y0_sum, add_up)
                nc.scalar.activation(y_stage[:, g % 2], y_psum(g % 2), ACT.Identity,
                                     bias=cols[:, R_B2 + g:R_B2 + g + 1]).then_inc(y_staged, 1)
                act.wait_ge(y_staged, G * i + g + 1)
                act.sem_inc(y_psum_free, 1)

            def body(i, kind):
                start, last = kind == FIRST, kind == LAST
                slot, _ = PLAN[kind]
                for k in range(K):
                    g = k // C
                    if ("T", g + 1) in slot and k % C == 0:
                        act.wait_ge(xlo_done, G * i + g + 1)
                        copy_xT(G * i + g + 1, slot["T", g + 1])
                        round_xT(G * i + g + 1, (g + 1) % G)
                    if last and k == K_MEAN:
                        act.wait_ge(y0_stat, 1)
                        nc.scalar.copy(stat[:], ring(slot["M", 0])[:, 0:TB]).then_inc(y0_mean, 1)
                    if last and k == K_VAR:
                        act.wait_ge(y0_stat, 2)
                        act.wait_ge(y0_centred, G)
                        nc.scalar.copy(stat[:], ring(slot["V", 0])[:, 0:TB]).then_inc(y0_var, 1)
                    if ("S", k + 2) in slot:
                        act.wait_ge(glo_done, K * i + k + 1)
                        gelu(K * i + k + 2, (k + 2) % K, slot["S", k + 2])
                    if last and k in K_SQ:
                        j = K_SQ.index(k)
                        act.wait_ge(y0_centred, 2 * j + 2)
                        if j == 0:
                            act.wait_ge(emb_chunk, KE + 1)
                        if j >= 2:
                            act.wait_ge(y0_sum, G + 2 * j - 3)
                        nc.scalar.activation(squares[:, 2 * (j % 2):2 * (j % 2) + 2], yb0[:, 2 * j:2 * j + 2],
                                             ACT.Square).then_inc(y0_squared, 1)
                    if last and k == K_VAR:
                        act.wait_ge(y0_var, 1)
                        nc.scalar.activation(stat[:], stat[:], ACT.Sqrt, bias=eps[:]).then_inc(y0_std, 1)
                        nc.scalar.preload_act_table(ACT.Gelu)
                    if start and k % C == 1 and g + 2 < G:
                        round_group(g + 2)
                    if kind == MIDDLE and k % PERIOD in AT_ROUND:
                        p = PERIODS * i - PERIODS + k // PERIOD
                        s = AT_ROUND.index(k % PERIOD)
                        act.wait_ge(wraw_landed[s], landed(G - 2 + s) + 16 * (p + 1))
                        nc.scalar.copy(oW_hi[:, 2 * p + s], wraw[:, s]).then_inc(aw_hi_done, 1)
                    if k % C == C - 1 and not (last and g == G - 1):
                        stage_y(i, g, g - 1 if start and g >= 2 else G if kind == MIDDLE and g < 2 else None)

            body(0, FIRST)
            with act.Fori(1, NA - 1) as i:
                body(i, MIDDLE)
            body(NA - 1, LAST)
            nc.scalar.preload_act_table(ACT.Silu)

            def silu_group(s, b, g):
                return nc.scalar.activation(yb[s][:, g], yb[s][:, g], ACT.Silu,
                                            scale=mod_a[:, b, g:g + 1], bias=mod_c[:, b, g:g + 1])

            act.wait_ge(mod_step, 5)
            for g in range(G):
                if g == HG:
                    stage_y(NA - 1, G - 1)
                act.wait_ge(y0_normed, g + 1)
                silu_group(0, 0, g).then_inc(y0_silu, 1)

            def norm(i, s, b):
                for h in range(2):
                    half = slice(h * HG, (h + 1) * HG)
                    act.wait_ge(centred, 2 * i + h + 1)
                    nc.scalar.activation(sq[:, half], yb[s][:, half], ACT.Square).then_inc(squared, 1)
                nc.scalar.preload_act_table(ACT.Sqrt)
                act.wait_ge(stat_psum, 2 * i + 2)
                nc.scalar.activation(stat[:], var_ps, ACT.Sqrt, bias=eps[:]).then_inc(std_done, 1)
                nc.scalar.preload_act_table(ACT.Silu)
                for g in range(G):
                    if g % HG == 0:
                        act.wait_ge(normed, 2 * i + g // HG + 1)
                    silu_group(s, b, g).then_inc(silu_done, 1)

            with act.Fori(0, NB // 2 - 1) as j:
                norm(2 * j, 1, j)
                norm(2 * j + 1, 0, j + 1)
            norm(NB - 2, 1, NB // 2 - 1)

        @block.vector
        def _(dve):
            nc.vector.memset(stat[:, 0:P], 1.0 / D).then_inc(ones_set, 1)
            nc.vector.memset(eps[:], LN_EPS).then_inc(ones_set, 1)
            nc.vector.memset(cond_silu[:], 0.0).then_inc(cond_zeroed, 1)
            dve.wait_ge(ones_set, 2)
            nc.vector.tensor_copy(ones_r[:], stat[:, 0:P]).then_inc(ones_ready, 1)
            def split_w0(j):
                dve.wait_ge(wraw_landed[0] if j else w1_landed, 16)
                raw = wraw[:, 0, j * FF:(j + 1) * FF]
                nc.vector.tensor_copy(W[:, 0, 2 * j], raw).then_inc(w_hi_done, 1)
                dve.wait_ge(w_hi_done, j + 1)
                nc.vector.tensor_tensor(W[:, 0, 2 * j + 1], raw, W[:, 0, 2 * j].bitcast(F32), ALU.subtract
                                        ).then_inc(w_split0, 1)

            split_w0(0)
            for h in range(2):
                part = slice(h * BANK, (h + 1) * BANK)
                dve.wait_ge(xhi_done if h else x0_hi, 1)
                nc.vector.tensor_tensor(xT_lo[:, 0, part], xT_raw[:, part], xT_hi[:, 0, part].bitcast(F32),
                                        ALU.subtract).then_inc(xlo_done if h else x0_lo, 1)
                if h == 0:
                    dve.wait_ge(vec_turned, 1)
                    nc.vector.tensor_copy(cols[:], psum[:, 4, 0:ROWS]).then_inc(cols_ready, 1)
            split_w0(1)

            def rest_xT(n, g):
                dve.wait_ge(xhi_done, n + 1)
                nc.vector.tensor_tensor(xT_lo[:, g % 2], xT_raw[:], xT_hi[:, g % 2].bitcast(F32),
                                        ALU.subtract).then_inc(xlo_done, 1)

            def split_gelu(m, s):
                dve.wait_ge(gelu_done, m + 1)
                nc.vector.tensor_copy(g_hi[:, s], g_raw[:, s]).then_inc(ghi_done, 1)
                dve.wait_ge(ghi_done, m + 1)
                nc.vector.tensor_tensor(g_lo[:, s], g_raw[:, s], g_hi[:, s].bitcast(F32),
                                        ALU.subtract).then_inc(glo_done, 1)

            def modulation():
                dve.wait_ge(emb_copied, KE + 2)
                nc.vector.tensor_tensor(emb[:], emb[:], cols[:, R_EB:R_EB + NE].unsqueeze(2).to_broadcast([P, NE, B]),
                                        ALU.add).then_inc(mod_step, 1)
                dve.wait_ge(mod_step, 1)
                scale = emb[:, 0:G].rearrange("p g b -> p b g")
                shift = emb[:, G:NE].rearrange("p g b -> p b g")
                g_all = cols[:, R_G:R_G + G].unsqueeze(1).to_broadcast([P, B, G])
                b_all = cols[:, R_B:R_B + G].unsqueeze(1).to_broadcast([P, B, G])
                nc.vector.tensor_scalar(mod_t[:], scale, 1.0, None, ALU.add).then_inc(mod_step, 1)
                dve.wait_ge(mod_step, 2)
                nc.vector.tensor_tensor(mod_a[:], mod_t[:], g_all, ALU.mult).then_inc(mod_step, 1)
                nc.vector.tensor_tensor(mod_c[:], mod_t[:], b_all, ALU.mult).then_inc(mod_step, 1)
                dve.wait_ge(mod_step, 4)
                nc.vector.tensor_tensor(mod_c[:], mod_c[:], shift, ALU.add).then_inc(mod_step, 1)

            split_gelu(0, 0)
            split_gelu(1, 1)
            nc.vector.memset(emb_rows[:], 0.0).then_inc(emb_copied, 1)

            def body(i, kind):
                last = kind == LAST
                slot, _ = PLAN[kind]
                for k in range(K):
                    g = k // C
                    if kind == MIDDLE and k in K_EMB:
                        n = K_EMB.index(k)
                        r = E_PER_BLOCK * i - E_PER_BLOCK + n
                        dve.wait_ge(emb_chunk, r + 2)
                        dve.wait_ge(emb_copied, r + 1)
                        nc.vector.tensor_tensor(emb_rows[:], ring(slot["E", n])[:, 0:BANK], emb_rows[:], ALU.add
                                                ).then_inc(emb_copied, 1)
                    if last and k == K_TURN:
                        dve.wait_ge(emb_turned, 1)
                        ps = ring(slot["F", 0])[:, 0:BANK].rearrange("p (c j m) -> p j c m", c=4, j=4)
                        nc.vector.tensor_copy(emb[:].rearrange("p (j c) b -> p j c b", j=4), ps[:, :, :, 0:B]
                                              ).then_inc(emb_copied, 1)
                    if ("T", g + 1) in slot and k % C == 0:
                        rest_xT(G * i + g + 1, (g + 1) % G)
                    if ("S", k + 2) in slot:
                        dve.wait_ge(s2_done, K * i + k + 1)
                        split_gelu(K * i + k + 2, k % 2)
                    if last and k in K_INV:
                        dve.wait_ge(y0_std, 1)
                        cuts = (0, 160, 336, TB)
                        n = K_INV.index(k)
                        piece = slice(cuts[n], cuts[n + 1])
                        nc.vector.reciprocal(stat[:, piece], stat[:, piece]).then_inc(y0_rstd, 1)
                    if last and k == K_TURN + 2:
                        modulation()

            body(0, FIRST)
            with dve.Fori(1, NA - 1) as i:
                body(i, MIDDLE)
            body(NA - 1, LAST)

            for n, part in enumerate(Y0_PARTS):
                dve.wait_ge(y0_silu, part.stop)
                nc.vector.tensor_copy(s_hi0[:, part], yb0[:, part]).then_inc(y0_shi, 1)
                dve.wait_ge(y0_shi, n + 1)
                nc.vector.tensor_tensor(s_lo0[:, part], yb0[:, part], s_hi0[:, part].bitcast(F32),
                                        ALU.subtract).then_inc(y0_slo, 1)

            def group_sum(n, src):
                nc.vector.tensor_tensor(sq[:, 0:4], src[:, 0:4], src[:, 4:8], ALU.add).then_inc(tree, 1)
                dve.wait_ge(tree, 3 * n + 1)
                nc.vector.tensor_tensor(sq[:, 0:2], sq[:, 0:2], sq[:, 2:4], ALU.add).then_inc(tree, 1)
                dve.wait_ge(tree, 3 * n + 2)
                nc.vector.tensor_tensor(stat[:], sq[:, 0], sq[:, 1], ALU.add).then_inc(tree, 1)
                dve.wait_ge(tree, 3 * n + 3)
                nc.vector.tensor_copy(sum_hi[:], stat[:]).then_inc(sum_split, 1)
                dve.wait_ge(sum_split, 2 * n + 1)
                nc.vector.tensor_tensor(sum_lo[:], stat[:], sum_hi[:].bitcast(F32), ALU.subtract
                                        ).then_inc(sum_split, 1)

            def finish(i, t):
                dve.wait_ge(proj_done, SB * i + t + 1)
                dve.wait_ge(res_biased, SB * i + t + 1)
                nc.vector.tensor_tensor(res[:, t % 2], proj[t % 2], res[:, t % 2], ALU.add
                                        ).then_inc(out_ready, 1)

            def centre(i, s, h):
                half = yb[s][:, h * HG:(h + 1) * HG]
                nc.vector.tensor_tensor(half, half, mean_ps.unsqueeze(1).to_broadcast([P, HG, TB]),
                                        ALU.subtract).then_inc(centred, 1)

            def normalise(i, s, h):
                half = yb[s][:, h * HG:(h + 1) * HG]
                nc.vector.tensor_tensor(half, half, stat[:].unsqueeze(1).to_broadcast([P, HG, TB]),
                                        ALU.mult).then_inc(normed, 1)

            def split_silu(i, s, h):
                half = slice(h * HG, (h + 1) * HG)
                dve.wait_ge(silu_done, G * i + (h + 1) * HG)
                nc.vector.tensor_copy(s_hi[s][:, half], yb[s][:, half]).then_inc(shi_done, 1)
                dve.wait_ge(shi_done, 2 * i + h + 1)
                nc.vector.tensor_tensor(s_lo[s][:, half], yb[s][:, half], s_hi[s][:, half].bitcast(F32),
                                        ALU.subtract).then_inc(slo_done, 1)

            def window(i, s, landed, last):
                if last:
                    for t in range(SB - 1):
                        finish(i, t)
                    dve.wait_ge(res_biased, SB * NB)
                    for h in range(2):
                        part = slice(h * BANK, (h + 1) * BANK)
                        dve.wait_ge(proj_done, SB * NB + h)
                        nc.vector.tensor_tensor(res[:, 1, part], proj[1][:, part], res[:, 1, part], ALU.add
                                                ).then_inc(out_ready, 1)
                    return
                dve.wait_ge(y_landed[s], 16 * landed)
                group_sum(2 * i, yb[s])
                dve.wait_ge(stat_psum, 2 * i + 1)
                centre(i, s, 0)
                centre(i, s, 1)
                finish(i, 0)
                dve.wait_ge(squared, 2 * i + 2)
                group_sum(2 * i + 1, sq)
                finish(i, 1)
                dve.wait_ge(std_done, i + 1)
                nc.vector.reciprocal(stat[:], stat[:]).then_inc(rstd_done, 1)
                dve.wait_ge(rstd_done, i + 1)
                normalise(i, s, 0)
                normalise(i, s, 1)
                split_silu(i, s, 0)
                finish(i, 2)
                split_silu(i, s, 1)
                finish(i, 3)

            dve.wait_ge(s2_done, K * NA)
            with dve.Fori(0, NB // 2 - 1) as j:
                window(2 * j, 1, j + 1, False)
                window(2 * j + 1, 0, j + 1, False)
            window(NB - 2, 1, NB // 2, False)
            window(NB - 1, 0, 0, True)

        @block.tensor
        def _(pe):
            def turn_x(slot, g):
                for s in range(SUB):
                    mm = nc.tensor.transpose(ring(slot)[:, s * P:(s + 1) * P], xin[:, g % 2, s], ident[:])
                mm.then_inc(xT_psum, 1)

            def first(k, slot, low_part=None):
                g, c = k // C, k % C
                cut = slice(c * P, (c + 1) * P)
                for n, (w, v) in enumerate(((W1_HI, xT_hi), (W1_LO, xT_hi), (W1_HI, xT_lo))):
                    if n == 2 and low_part is not None:
                        pe.wait_ge(xlo_done, low_part)
                    for h in range(2):
                        mm = nc.tensor.matmul(ring(slot)[:, h * BANK:(h + 1) * BANK], W[:, g, w, cut],
                                              v[:, g % 2, h * BANK:(h + 1) * BANK],
                                              start=(n == 0), stop=(n == 2))
                mm.then_inc(s1_done, 1)

            def second(k, m):
                g, c = k // C, k % C
                cut = slice(c * P, (c + 1) * P)
                pe.wait_ge(ghi_done, m + 1)
                for n, (w, v) in enumerate(((W2_HI, g_hi), (W2_LO, g_hi), (W2_HI, g_lo))):
                    if n == 2:
                        pe.wait_ge(glo_done, m + 1)
                    for h in range(2):
                        mm = nc.tensor.matmul(y_psum(g % 2)[:, h * BANK:(h + 1) * BANK], W[:, g, w, cut],
                                              v[:, k % 2, h * BANK:(h + 1) * BANK],
                                              start=(c == 0 and n == 0), stop=(c == C - 1 and n == 2))
                mm.then_inc(s2_done, 1)

            def mean_of_sum(ps):
                nc.tensor.matmul(ps, ones_r[:], sum_hi[:], start=True, stop=False)
                return nc.tensor.matmul(ps, ones_r[:], sum_lo[:], start=False, stop=True)

            def embed(r, q, ps):
                pe.wait_ge(emb_landed, 16 * (r + 1))
                for j in range(4):
                    mm = nc.tensor.matmul(ps[32 * j:32 * j + 32, 0:BANK], cond_now[:, q],
                                          wraw[:].rearrange("p s q -> p (s q)")[:, j * BANK:(j + 1) * BANK],
                                          start=True, stop=True, tile_position=(0, 32 * j))
                mm.then_inc(emb_chunk, 1)

            pe.wait_ge(ident_ready, 1)
            for h in range(2):
                pe.wait_ge(x0_landed[h], 16)
                for s in range(h * SB, (h + 1) * SB):
                    mm = nc.tensor.transpose(ring(0)[:, s * P:(s + 1) * P], xin[:, 0, s], ident[:])
                mm.then_inc(xT_psum if h else x0T_psum, 1)
            pe.wait_ge(vec_landed, 16 * 3)
            pe.wait_ge(vec_landed_pool, 16 * 3)
            nc.tensor.transpose(psum[:, 4, 0:ROWS], vec_rows[0:ROWS, :], ident[0:ROWS, 0:ROWS]
                                ).then_inc(vec_turned, 1)
            pe.wait_ge(w_split0, 1)
            for h in range(2):
                part = slice(h * BANK, (h + 1) * BANK)
                for n, (w, v) in enumerate(((W1_HI, xT_hi), (W1_LO, xT_hi), (W1_HI, xT_lo))):
                    if n == 0:
                        pe.wait_ge(xhi_done if h else x0_hi, 1)
                    if n == 2:
                        pe.wait_ge(xlo_done if h else x0_lo, 1)
                    mm = nc.tensor.matmul(ring(1)[:, part], W[:, 0, w, 0:P], v[:, 0, part],
                                          start=(n == 0), stop=(n == 2))
            mm.then_inc(s1_done, 1)
            first(1, 0)

            def body(i, kind):
                start, last = kind == FIRST, kind == LAST
                slot, before = PLAN[kind]

                def take(use):
                    kind, n = before[use]
                    if kind == "S":
                        pe.wait_ge(gelu_done, K * i + n + 1)
                    elif kind == "T":
                        pe.wait_ge(xraw_done, G * i + n + 1)
                    elif kind == "E":
                        pe.wait_ge(emb_copied, E_PER_BLOCK * i - E_PER_BLOCK + n + 2)
                    elif kind == "F":
                        pe.wait_ge(emb_copied, KE + 2)
                    else:
                        pe.wait_ge({"M": y0_mean, "V": y0_var}[kind], 1)
                    return slot[use]

                for k in range(K):
                    g = k // C
                    if k % C == 0 and ("T", g + 1) in slot:
                        if g + 1 < G:
                            pe.wait_ge(x_landed[(g + 1) % 2], 16 * ((G // 2) * i + g // 2 + 1))
                        else:
                            pe.wait_ge(x_landed[0], 16 * ((G // 2) * i + G // 2))
                        turn_x(take(("T", g + 1)), (g + 1) % G)
                    if kind == MIDDLE and k in K_EMB:
                        n = K_EMB.index(k)
                        ps = ring(take(("E", n)))
                        if n % 2 == 0:
                            pe.wait_ge(cond_now_ready, PERIODS * i - PERIODS + n // 2 + 1)
                        embed(E_PER_BLOCK * i - E_PER_BLOCK + n, n % 2, ps)
                    if last and k == K_TURN:
                        ps = ring(take(("F", 0)))
                        pe.wait_ge(emb_copied, KE + 1)
                        for c in range(4):
                            mm = nc.tensor.transpose(ps[:, c * P:(c + 1) * P], emb_rows[:, c * P:(c + 1) * P],
                                                     ident[:])
                        mm.then_inc(emb_turned, 1)
                    if last and k == K_MEAN:
                        s = take(("M", 0))
                        pe.wait_ge(y0_split, 2)
                        mean_of_sum(ring(s)[:, 0:TB]).then_inc(y0_stat, 1)
                    if last and k == K_VAR:
                        s = take(("V", 0))
                        pe.wait_ge(y0_split, 4)
                        mean_of_sum(ring(s)[:, 0:TB]).then_inc(y0_stat, 1)
                    if ("S", k + 2) in slot:
                        s = take(("S", k + 2))
                        if k % C == C - 2:
                            pe.wait_ge(xhi_done, G * i + g + 2)
                            if start and g + 1 < G:
                                pe.wait_ge(pw_split, 2 * (g + 1))
                        first((k + 2) % K, s, G * i + g + 2 if k % C == C - 2 else None)
                    if k % C == 0:
                        pe.wait_ge(y_psum_free, G * i + g + 1)
                    second(k, K * i + k)

            pe.wait_ge(ones_ready, 1)
            pe.wait_ge(w_split0, 2)
            body(0, FIRST)
            with pe.Fori(1, NA - 1) as i:
                body(i, MIDDLE)
            body(NA - 1, LAST)

            def project(s, t, g, low_part=None):
                cut = slice(t * P, (t + 1) * P)
                for n, (v, w) in enumerate(((s_hi[s], oW_hi), (s_hi[s], oW_lo), (s_lo[s], oW_hi))):
                    if n == 2 and low_part is not None:
                        pe.wait_ge(y0_slo, low_part)
                    for h in range(2):
                        mm = nc.tensor.matmul(proj[t % 2][:, h * BANK:(h + 1) * BANK], v[:, g, cut],
                                              w[:, g, h * BANK:(h + 1) * BANK],
                                              start=(g == 0 and n == 0), stop=(g == G - 1 and n == 2))
                if g == G - 1:
                    mm.then_inc(proj_done, 1)

            def project_halves(s, t):
                cut = slice(t * P, (t + 1) * P)
                for h in range(2):
                    part = slice(h * BANK, (h + 1) * BANK)
                    for g in range(G):
                        for n, (v, w) in enumerate(((s_hi[s], oW_hi), (s_hi[s], oW_lo), (s_lo[s], oW_hi))):
                            mm = nc.tensor.matmul(proj[t % 2][:, part], v[:, g, cut], w[:, g, part],
                                                  start=(g == 0 and n == 0), stop=(g == G - 1 and n == 2))
                    mm.then_inc(proj_done, 1)

            def window(i, s, first, last):
                at_mean, at_var = ((1, 1), (2, 3)) if first else ((0, 6), (2, 0))
                for t in range(SB):
                    if not (first and t < 2):
                        pe.wait_ge(out_ready, SB * i + t - 1)
                    if last and t == SB - 1:
                        project_halves(s, t)
                        continue
                    for g in range(G):
                        low_part = None
                        for n, part in enumerate(Y0_PARTS):
                            if t == 0 and first and g == part.start:
                                pe.wait_ge(y0_shi, n + 1)
                                low_part = n + 1
                        if t == 0 and not first and g % HG == 0:
                            pe.wait_ge(slo_done, 2 * i - 2 + g // HG + 1)
                        project(s, t, g, low_part)
                        if (t, g) == at_mean and not last:
                            if first:
                                pe.wait_ge(y_psum_free, NA * G + 2)
                            pe.wait_ge(sum_split, 4 * i + 2)
                            mean_of_sum(mean_ps).then_inc(stat_psum, 1)
                        if (t, g) == at_var and not last:
                            pe.wait_ge(sum_split, 4 * i + 4)
                            mean_of_sum(var_ps).then_inc(stat_psum, 1)

            window(0, 0, True, False)
            window(1, 1, False, False)
            with pe.Fori(1, NB // 2 - 1) as j:
                window(2 * j, 0, False, False)
                window(2 * j + 1, 1, False, False)
            window(NB - 2, 0, False, False)
            window(NB - 1, 1, False, True)


_INS = ["x", "cond_2048", "L0_cond_W1", "L0_cond_b1", "L0_cond_W2", "L0_cond_b2", "L0_cond_emb_W",
        "L0_cond_emb_b", "L0_cond_ln_g", "L0_cond_ln_b", "L0_cond_out_W", "L0_cond_out_b"]


def kernel(**inputs):
    import numpy as _np
    import concourse.bacc as _bacc
    from concourse import mybir as _mybir
    from concourse.bass_utils import run_bass_kernel_spmd as _run

    nc = _bacc.Bacc("TRN2", target_bir_lowering=False, num_devices=1)
    arrays, args = {}, []
    for name in _INS:
        a = _np.ascontiguousarray(inputs[name])
        arrays[f"in_{name}"] = a
        args.append(nc.dram_tensor(f"in_{name}", a.shape, _mybir.dt.from_np(a.dtype), kind="ExternalInput").ap())
    args.append(nc.dram_tensor("out", arrays["in_x"].shape, F32, kind="ExternalOutput").ap())
    cond_ffn_program(nc, *args)
    r = _run(nc, [arrays], core_ids=[0])
    return r.results[0]["out"]
```
